# Optimizing a Trainium2 kernel written in Bass

```python
import numpy as np
import jax
import jax.numpy as jnp

def _softmax(x, axis=-1):
    return jax.nn.softmax(x, axis=axis)

def _gelu(x):
    return jax.nn.gelu(x, approximate=True)

def _silu(x):
    return jax.nn.silu(x)

def _sigmoid(x):
    return jax.nn.sigmoid(x)

def _layernorm(x, axis=-1, eps=1e-05):
    m = jnp.mean(x, axis=axis, keepdims=True)
    v = jnp.var(x, axis=axis, keepdims=True)
    return (x - m) / jnp.sqrt(v + eps)

def _scatter_add(tgt, idx, src, axis=0):
    return tgt.at[idx].add(src)

def _segment_sum(src, seg, n):
    return jax.ops.segment_sum(src, seg, n)
kernel_name = 'mk_flamingo_gated_d1_seqx_r4_28e059'

def setup_inputs(seed: int=0):
    np.random.seed(seed)
    _w = jnp.asarray

    def _rec_inputs():
        import jax
        import jax.numpy as jnp
        _rk = jax.random.key(seed)
        x = 0.000341 + 1 * jax.random.normal(jax.random.fold_in(_rk, 1), (16, 256, 512), jnp.float32)
        _lenS = 256 - jax.random.randint(jax.random.fold_in(_rk, 7), (16,), 0, max(1, 256 // 4) + 1, jnp.int32)
        _lenS2 = 256 - jax.random.randint(jax.random.fold_in(_rk, 8), (16,), 0, max(1, 256 // 4) + 1, jnp.int32)
        _ctx_2048P = jax.random.normal(jax.random.fold_in(_rk, 11), (16, 16, 512), jnp.float32)
        _ctx_2048c = jax.random.dirichlet(jax.random.fold_in(_rk, 511), 0.3 * jnp.ones((16,), jnp.float32), (16, 256))
        _ctx_2048t = jnp.einsum('bsk,bkd->bsd', _ctx_2048c, _ctx_2048P)
        _ctx_2048t = _ctx_2048t * jax.lax.rsqrt(jnp.mean(jnp.square(_ctx_2048t)) + 1e-12) * 0.953939
        ctx_2048 = -1.47943e-05 + 1.00017 * (_ctx_2048t + 0.3 * jax.random.normal(jax.random.fold_in(_rk, 611), (16, 256, 512), jnp.float32))
        _g = jax.random.normal(jax.random.fold_in(_rk, 9001), (2, 1), jnp.float32)
        _g = jnp.sign(_g) * jnp.maximum(jnp.abs(_g), 1.0) + (_g == 0) * 1.0
        g_xattn = _g[0]
        g_ffn = _g[1]
        return (x, ctx_2048, g_xattn, g_ffn)
    x, ctx_2048, g_xattn, g_ffn = _rec_inputs()

    def _L0_xattn_setup():
        import jax, jax.numpy as jnp
        import numpy as np

        def _wkv(time_decay, time_first, k, v):
            w = -jnp.exp(time_decay)
            u = time_first
            B, T, C = k.shape
            aa = jnp.zeros((B, C), dtype=k.dtype)
            bb = jnp.zeros((B, C), dtype=k.dtype)
            pp = jnp.full((B, C), -1e+38, dtype=k.dtype)

            def step(carry, kv_t):
                aa, bb, pp = carry
                kt, vt = kv_t
                ww = u + kt
                q = jnp.maximum(pp, ww)
                e1 = jnp.exp(pp - q)
                e2 = jnp.exp(ww - q)
                y_t = (e1 * aa + e2 * vt) / (e1 * bb + e2)
                ww2 = pp + w
                q2 = jnp.maximum(ww2, kt)
                e1b = jnp.exp(ww2 - q2)
                e2b = jnp.exp(kt - q2)
                new_carry = (e1b * aa + e2b * vt, e1b * bb + e2b, q2)
                return (new_carry, y_t)
            ks = jnp.transpose(k, (1, 0, 2))
            vs = jnp.transpose(v, (1, 0, 2))
            _, ys = jax.lax.scan(step, (aa, bb, pp), (ks, vs))
            return jnp.transpose(ys, (1, 0, 2))
        key = jax.random.key(seed)
        k1, k2, k3, k4 = jax.random.split(key, 4)
        B, T, C = (8, 256, 512)
        return {'batch_size': B, 'seq_len': T, 'embedding_dim': C, 'time_decay': jax.random.normal(k1, (C,), dtype=jnp.float32), 'time_first': jax.random.normal(k2, (C,), dtype=jnp.float32), 'k': jax.random.normal(k3, (B, T, C), dtype=jnp.float32), 'v': jax.random.normal(k4, (B, T, C), dtype=jnp.float32)}
    _L0_xattn_all = _L0_xattn_setup()
    _L0_xattn_in = {k: v for k, v in _L0_xattn_all.items() if k in ('time_decay', 'time_first')}
    del _L0_xattn_all

    def _L0_ffn_setup():
        import jax, jax.numpy as jnp
        import numpy as np
        B, S, D = (4, 1024, 512)
        E, K, I, J = (8, 2, 352, 1408)
        CAP_FACTOR = 1.25
        STD = 0.02

        def _moe_routed(x_flat, router, w_up_gate, w_down):
            T, d = x_flat.shape
            logits = jnp.einsum('td,de->te', x_flat, router)
            topk_logits, sel = jax.lax.top_k(logits, K)
            cw = jax.nn.softmax(topk_logits, axis=-1).astype(x_flat.dtype)
            C = int(np.ceil(T * K / E * CAP_FACTOR))
            e_flat = sel.reshape(-1)
            oh = jax.nn.one_hot(e_flat, E, dtype=jnp.int32)
            pos_all = jnp.cumsum(oh, axis=0) - oh
            pos = jnp.take_along_axis(pos_all, e_flat[:, None], axis=1)[:, 0]
            valid = pos < C
            safe_pos = jnp.where(valid, pos, C)
            tok = jnp.repeat(jnp.arange(T), K)
            buf = jnp.zeros((E, C, d), x_flat.dtype).at[e_flat, safe_pos].set(x_flat[tok], mode='drop')
            gate_up = jnp.einsum('ecd,edm->ecm', buf, w_up_gate)
            gate, up = jnp.split(gate_up, [I], axis=-1)
            h = jax.nn.silu(gate) * up
            out_buf = jnp.einsum('eci,eid->ecd', h, w_down)
            gathered = out_buf[e_flat, jnp.minimum(safe_pos, C - 1)]
            gathered = gathered * valid[:, None].astype(x_flat.dtype)
            w = cw.reshape(-1)
            y = jnp.zeros((T, d), x_flat.dtype).at[tok].add(w[:, None] * gathered)
            return y

        def _shared_mlp(x_flat, shared_w_up_gate, shared_w_down):
            gu = jnp.einsum('td,dm->tm', x_flat, shared_w_up_gate)
            gate, up = jnp.split(gu, [J], axis=-1)
            return jnp.einsum('tm,md->td', jax.nn.silu(gate) * up, shared_w_down)
        key = jax.random.key(seed)
        kx, kr, ku, kd, ksu, ksd = jax.random.split(key, 6)
        x = jax.random.normal(kx, (B, S, D), dtype=jnp.float32)
        router = STD * jax.random.truncated_normal(kr, -3, 3, (D, E), dtype=jnp.float32)
        w_up_gate = STD * jax.random.truncated_normal(ku, -3, 3, (E, D, 2 * I), dtype=jnp.float32)
        w_down = STD * jax.random.truncated_normal(kd, -3, 3, (E, I, D), dtype=jnp.float32)
        shared_w_up_gate = STD * jax.random.truncated_normal(ksu, -3, 3, (D, 2 * J), dtype=jnp.float32)
        shared_w_down = STD * jax.random.truncated_normal(ksd, -3, 3, (J, D), dtype=jnp.float32)
        return {'x': x, 'router': router, 'w_up_gate': w_up_gate, 'w_down': w_down, 'shared_w_up_gate': shared_w_up_gate, 'shared_w_down': shared_w_down}
    _L0_ffn_all = _L0_ffn_setup()
    _L0_ffn_in = {k: v for k, v in _L0_ffn_all.items() if k in ('router', 'w_up_gate', 'w_down', 'shared_w_up_gate', 'shared_w_down')}
    del _L0_ffn_all
    return {'x': x, 'ctx_2048': ctx_2048, 'g_xattn': g_xattn, 'g_ffn': g_ffn, 'L0_xattn_time_decay': _L0_xattn_in['time_decay'], 'L0_xattn_time_first': _L0_xattn_in['time_first'], 'L0_ffn_router': _L0_ffn_in['router'], 'L0_ffn_w_up_gate': _L0_ffn_in['w_up_gate'], 'L0_ffn_w_down': _L0_ffn_in['w_down'], 'L0_ffn_shared_w_up_gate': _L0_ffn_in['shared_w_up_gate'], 'L0_ffn_shared_w_down': _L0_ffn_in['shared_w_down']}

def reference(x, ctx_2048, g_xattn, g_ffn, L0_xattn_time_decay, L0_xattn_time_first, L0_ffn_router, L0_ffn_w_up_gate, L0_ffn_w_down, L0_ffn_shared_w_up_gate, L0_ffn_shared_w_down):
    import jax
    import jax.numpy as jnp

    def _L0_xattn_ref(batch_size, seq_len, embedding_dim, time_decay, time_first, k, v):
        import jax, jax.numpy as jnp
        import numpy as np

        def _wkv(time_decay, time_first, k, v):
            w = -jnp.exp(time_decay)
            u = time_first
            B, T, C = k.shape
            aa = jnp.zeros((B, C), dtype=k.dtype)
            bb = jnp.zeros((B, C), dtype=k.dtype)
            pp = jnp.full((B, C), -1e+38, dtype=k.dtype)

            def step(carry, kv_t):
                aa, bb, pp = carry
                kt, vt = kv_t
                ww = u + kt
                q = jnp.maximum(pp, ww)
                e1 = jnp.exp(pp - q)
                e2 = jnp.exp(ww - q)
                y_t = (e1 * aa + e2 * vt) / (e1 * bb + e2)
                ww2 = pp + w
                q2 = jnp.maximum(ww2, kt)
                e1b = jnp.exp(ww2 - q2)
                e2b = jnp.exp(kt - q2)
                new_carry = (e1b * aa + e2b * vt, e1b * bb + e2b, q2)
                return (new_carry, y_t)
            ks = jnp.transpose(k, (1, 0, 2))
            vs = jnp.transpose(v, (1, 0, 2))
            _, ys = jax.lax.scan(step, (aa, bb, pp), (ks, vs))
            return jnp.transpose(ys, (1, 0, 2))
        assert seq_len <= 256
        return _wkv(time_decay, time_first, k, v)

    def _L0_ffn_ref(x, router, w_up_gate, w_down, shared_w_up_gate, shared_w_down):
        import jax, jax.numpy as jnp
        import numpy as np
        B, S, D = (4, 1024, 512)
        E, K, I, J = (8, 2, 352, 1408)
        CAP_FACTOR = 1.25
        STD = 0.02

        def _moe_routed(x_flat, router, w_up_gate, w_down):
            T, d = x_flat.shape
            logits = jnp.einsum('td,de->te', x_flat, router)
            topk_logits, sel = jax.lax.top_k(logits, K)
            cw = jax.nn.softmax(topk_logits, axis=-1).astype(x_flat.dtype)
            C = int(np.ceil(T * K / E * CAP_FACTOR))
            e_flat = sel.reshape(-1)
            oh = jax.nn.one_hot(e_flat, E, dtype=jnp.int32)
            pos_all = jnp.cumsum(oh, axis=0) - oh
            pos = jnp.take_along_axis(pos_all, e_flat[:, None], axis=1)[:, 0]
            valid = pos < C
            safe_pos = jnp.where(valid, pos, C)
            tok = jnp.repeat(jnp.arange(T), K)
            buf = jnp.zeros((E, C, d), x_flat.dtype).at[e_flat, safe_pos].set(x_flat[tok], mode='drop')
            gate_up = jnp.einsum('ecd,edm->ecm', buf, w_up_gate)
            gate, up = jnp.split(gate_up, [I], axis=-1)
            h = jax.nn.silu(gate) * up
            out_buf = jnp.einsum('eci,eid->ecd', h, w_down)
            gathered = out_buf[e_flat, jnp.minimum(safe_pos, C - 1)]
            gathered = gathered * valid[:, None].astype(x_flat.dtype)
            w = cw.reshape(-1)
            y = jnp.zeros((T, d), x_flat.dtype).at[tok].add(w[:, None] * gathered)
            return y

        def _shared_mlp(x_flat, shared_w_up_gate, shared_w_down):
            gu = jnp.einsum('td,dm->tm', x_flat, shared_w_up_gate)
            gate, up = jnp.split(gu, [J], axis=-1)
            return jnp.einsum('tm,md->td', jax.nn.silu(gate) * up, shared_w_down)
        b, s, d = x.shape
        x_flat = x.reshape(b * s, d)
        routed = _moe_routed(x_flat, router, w_up_gate, w_down)
        shared = _shared_mlp(x_flat, shared_w_up_gate, shared_w_down)
        return (routed + shared).reshape(b, s, d)
    x = x + jnp.tanh(g_xattn[0]) * _L0_xattn_ref(16, 256, 512, L0_xattn_time_decay, L0_xattn_time_first, _layernorm(x, axis=-1), ctx_2048)
    x = x + jnp.tanh(g_ffn[0]) * _L0_ffn_ref(_layernorm(x, axis=-1), L0_ffn_router, L0_ffn_w_up_gate, L0_ffn_w_down, L0_ffn_shared_w_up_gate, L0_ffn_shared_w_down)
    return x

_drawn_inputs = setup_inputs


def setup_inputs(seed=0):
    import zlib

    import numpy as np

    out = dict(_drawn_inputs(seed))
    spreads = {}
    factors = {'L0_ffn_router': 2.873}
    for name, (base, spread) in spreads.items():
        noise = np.random.default_rng([zlib.crc32(name.encode()), seed]).standard_normal(out[name].shape)
        drawn = base * np.exp(spread * noise) if base else spread * noise
        out[name] = jnp.asarray(drawn.astype(out[name].dtype))
    for name, factor in factors.items():
        out[name] = (out[name] * factor).astype(out[name].dtype)
    return out
```

```python
from contextlib import ExitStack

import concourse.bass as bass
from concourse import mybir

F32, F16, U32 = mybir.dt.float32, mybir.dt.float16, mybir.dt.uint32
ALU, ACT, AX = mybir.AluOpType, mybir.ActivationFunctionType, mybir.AxisListType

P = 128
BATCH, STEPS, D = 16, 256, 512
KT = D // P
Q = 4
TS = P // Q
QUADS = BATCH // Q
TPQ = STEPS // TS
TILES = QUADS * TPQ
GT = 4
GROUPS = TILES // GT
NTOK = TILES * P
HB = D // 32
SEG = TS + 1
E, TOPK, I, J = 8, 2, 352, 1408
CAP = -(-(NTOK * TOPK * 5) // (E * 4))
ET = CAP // P
CH = 256
EC = CAP // CH
IT = -(-I // P)
IM = [min(P, I - P * m) for m in range(IT)]
JT = J // P
EPS = 1e-5
WS = 2.0 ** 7
HS = 2.0 ** 4
TRASH = E * CAP
SLOTS = JT + GT
WCH = 2 * KT + IT
CONV = [[0, 1, 2], [3, 4, 5], [6, 7, 8], [9, 10], []]
TABS = 6
PMADE = 13
R_EXP, R_PREF, R_POS = 2, 20, 21


def build(nc, x, ctx_in, g_x, g_f, t_decay, t_first, router, w_ug, w_dn, s_ug, s_dn, out):
    es = ExitStack()
    with es:
        def sb(name, shape, dt):
            return es.enter_context(nc.sbuf_tensor(name, shape, dt))

        def pb(name, shape):
            return es.enter_context(nc.psum_tensor(name, shape, F32))

        def sem(name):
            return es.enter_context(nc.semaphore(name))

        xln_d = nc.dram_tensor("xln_d", (NTOK, D), F32, kind="Internal").ap()
        slot_out_d = nc.dram_tensor("slot_out_d", (E * CAP, D), F32, kind="Internal").ap()
        slot_tok_d = nc.dram_tensor("slot_tok_d", (TRASH + TOPK * NTOK, 1), F32, kind="Internal").ap()

        acc = sb("acc", [P, TILES * D], F32)
        wreg = sb("wreg", [P, JT * 3 * 1024], F16)
        hreg = sb("hreg", [P, JT * 2 * 512], F16)
        xT = sb("xT", [P, 2, 2, KT, 512], F16)
        srng = sb("srng", [P, 2, 512], F32)
        wkv = sb("wkv", [P, 7776], F32)
        sU = wreg[:, 0:JT * 2048].rearrange("p (m g h k c) -> p m g h k c", m=JT, g=2, h=2, k=KT)
        sD = wreg[:, JT * 2048:JT * 3072].rearrange("p (j h c) -> p j h c", j=JT, h=2)
        hh = hreg[:, :].rearrange("p (j h t) -> p j h t", j=JT, h=2)
        sst_u = hreg[:, 0:4 * 2048].bitcast(F32).rearrange("p (r g k c) -> p r g k c", r=4, g=2, k=KT)
        sst_d = hreg[:, 4 * 2048:4 * 2048 + 3 * 1024].bitcast(F32).rearrange("p (r c) -> p r c", r=3)

        at = [0]

        def carve(words):
            a = wkv[:, at[0]:at[0] + words]
            at[0] += words
            return a

        ctxb = [carve(D) for _ in range(2)]
        kbuf = carve(D)
        ek = carve(D)
        vT = carve(D)
        xln = [carve(D) for _ in range(2)]
        scan_in = carve(2 * HB * SEG).rearrange("p (n h s) -> p n h s", n=2, h=HB)
        scan_out = carve(2 * HB * SEG).rearrange("p (n h s) -> p n h s", n=2, h=HB)
        nd = carve(2 * D).rearrange("p (n h t) -> p n h t", n=2, h=HB)
        decay = carve(HB * SEG).rearrange("p (h s) -> p h s", h=HB)

        UW = 2 * 2 * KT * I
        EW = UW + IT * 2 * D
        ebuf = [wkv[:, 0:EW // 2].bitcast(F16), hreg[:, 0:EW]]
        eU = [b[:, 0:UW].rearrange("p (g h k c) -> p g h k c", g=2, h=2, k=KT) for b in ebuf]
        eD = [b[:, UW:EW].rearrange("p (j h c) -> p j h c", j=IT, h=2) for b in ebuf]
        at[0] = EW // 2
        wst = [carve(D) for _ in range(2)]
        eh = carve(2 * IT * CH).bitcast(F16).rearrange("p (r j h t) -> p r j h t", r=2, j=IT, h=2)
        xg1 = carve(D)
        assert at[0] <= 7776
        ostage = [hreg[:, EW + 1024 * r:EW + 1024 * (r + 1)].bitcast(F32) for r in range(2)]
        esr = [srng[:, 0, CH * r:CH * (r + 1)] for r in range(2)]
        xg = [xg1, srng[:, 1, :]]
        xgT = xT[:, 0, :, :, :].rearrange("p h k (r t) -> p r h k t", r=2)
        cg = [xT[:, r // 2, r % 2, :, :].rearrange("p k t -> p (k t)").bitcast(F32).rearrange(
            "p (n c) -> p n c", n=2)[:, :, :] for r in range(4)]

        tab_rows = srng[:, 1, 0:64].rearrange("p (n l) -> p n l", n=2)
        tab_cols = srng[:, 1, 64:128].rearrange("p (n h) -> p n h", n=2)
        ident = sb("ident", [P, P], F32)
        pref = sb("pref", [P, 4, P], F16)
        prefw = srng[:, 0, :].rearrange("p (m q r) -> p m q r", m=4, q=Q)
        iotae = sb("iotae", [P, E], F32)
        rowid = sb("rowid", [P, TILES], F32)
        e12 = sb("e12", [P, 2, HB], F32)
        gates = sb("gates", [P, 4], F32)
        mhalf = sb("mhalf", [P, 1], F32)
        rt_w = sb("rt_w", [P, 2, KT, E], F16)
        rt_f = sb("rt_f", [P, KT, E], F32)
        bn = sb("bn", [P, 2, 6], F32)
        mv = sb("mv", [P, 2, 2], F32)
        ve = sb("ve", [P, 2], F32)
        rstd = sb("rstd", [P, 2], F32)
        lt = sb("lt", [P, E], F32)
        top8 = sb("top8", [P, 8], F32)
        top8i = sb("top8i", [P, 8], U32)
        topv = sb("topv", [P, TILES * 2], F32)
        topi = sb("topi", [P, TILES * 2], F32)
        wcomb = sb("wcomb", [P, TOPK, TILES], F32)
        cslot = sb("cslot", [P, TILES * 2], U32)
        sslot = sb("sslot", [P, TILES * 2], U32)
        sidx = sb("sidx", [P, 2 * GT], U32)
        stok = sb("stok", [P, GT], F32)
        gidx = sb("gidx", [P, E * ET], U32)
        eidx = sb("eidx", [P, 2, ET], U32)

        rs = wkv[:, 0:3200]
        oh = rs[:, 0:2 * TILES * E].rearrange("p (n t e) -> p n t e", n=2, t=TILES)
        ohs = rs[:, 512:512 + 128].bitcast(F16)
        ohx = rs[:, 640:640 + 128].bitcast(F16)
        ohtot = rs[:, 768:768 + 128].bitcast(F16)
        ohrun = rs[:, 896:896 + 128].bitcast(F16)
        tot = rs[:, 1024:1024 + 32].rearrange("p (b e) -> p b e", b=QUADS)
        run = rs[:, 1056:1056 + 32].rearrange("p (b e) -> p b e", b=QUADS)
        pos = rs[:, 1088:1088 + 256].rearrange("p (t e) -> p t e", t=TILES)
        posk = rs[:, 1344:1344 + 64].rearrange("p (n t) -> p n t", n=2)
        valid = rs[:, 1408:1408 + 64].rearrange("p (n t) -> p n t", n=2)
        slot = rs[:, 1472:1472 + 64].rearrange("p (n t) -> p n t", n=2)
        trash = rs[:, 1536:1536 + 64].rearrange("p (n t) -> p n t", n=2)
        wtmp = rs[:, 1600:1600 + 64].rearrange("p (n t) -> p n t", n=2)
        sprod = rs[:, 1664:1664 + 512].rearrange("p (n t e) -> p n t e", n=2, t=TILES)
        tokt = rs[0:E * ET, 2176:2176 + 128]
        zslot = rs[0:E * ET, 2304:2304 + 128]

        PU = [[pb(f"PU{r}{g}", [P, 512]) for g in range(2)] for r in range(2)]
        PD = [pb(f"PD{r}", [P, 512]) for r in range(2)]
        PT = pb("PT", [P, 512])
        PR = pb("PR", [P, 512])

        dve_waits = sem("dve_waits"); pool_waits = sem("pool_waits")
        tab_zeroed = sem("tab_zeroed"); tab_in = sem("tab_in"); tab_turned = sem("tab_turned")
        const_in = sem("const_in"); pmade = sem("pmade"); tabs = sem("tabs")
        exps = sem("exps"); consts = sem("consts"); rhi = sem("rhi"); rlo = sem("rlo")
        in_loaded = [sem(f"in_loaded{r}") for r in range(2)]
        bn1 = sem("bn1"); var1 = sem("var1"); rstd1 = sem("rstd1")
        k_norm = sem("k_norm"); k_turned = sem("k_turned"); v_turned = sem("v_turned")
        ek_ready = sem("ek_ready"); pw = sem("pw"); scan_in_ready = sem("scan_in_ready"); nd_ready = sem("nd_ready")
        carried = sem("carried"); scanned = sem("scanned"); summed = sem("summed")
        rcp_done = sem("rcp_done"); y_done = sem("y_done"); y_turned = sem("y_turned"); x2_done = sem("x2_done")
        bn2 = sem("bn2"); var2 = sem("var2"); rstd2 = sem("rstd2"); xln_ready = sem("xln_ready")
        xln_stored = [sem(f"xln_stored{r}") for r in range(2)]
        x_turned = sem("x_turned"); xhi_ready = sem("xhi_ready"); xlo_ready = sem("xlo_ready")
        logits_ready = sem("logits_ready"); logits_taken = sem("logits_taken"); top_steps = sem("top_steps")
        wu_in = [sem(f"wu_in{r}") for r in range(4)]
        wd_in = [sem(f"wd_in{r}") for r in range(3)]
        wu_hi = sem("wu_hi"); wu_lo = sem("wu_lo"); wd_hi = sem("wd_hi"); wd_lo = sem("wd_lo")
        up_ready = sem("up_ready"); silu_done = sem("silu_done"); h_ready = sem("h_ready")
        hhi_ready = sem("hhi_ready"); hlo_ready = sem("hlo_ready")
        down_ready = sem("down_ready"); down_added = sem("down_added")
        rsteps = sem("rsteps"); pos_ready = sem("pos_ready"); routed = sem("routed")
        slots_zeroed = sem("slots_zeroed"); zeros_made = sem("zeros_made"); idx_copied = sem("idx_copied"); slots_sent = sem("slots_sent")
        slots_back = sem("slots_back"); slots_turned = sem("slots_turned"); gidx_ready = sem("gidx_ready")
        eidx_ready = sem("eidx_ready")
        gathered = [sem(f"gathered{r}") for r in range(2)]
        xg_turned = sem("xg_turned"); xg_hi = sem("xg_hi"); xg_lo = sem("xg_lo")
        ew_in = [sem(f"ew_in{r}") for r in range(2)]
        ew_hi = sem("ew_hi"); ew_lo = sem("ew_lo")
        eup_ready = sem("eup_ready"); esilu_done = sem("esilu_done"); eh_ready = sem("eh_ready")
        ehhi_ready = sem("ehhi_ready"); ehlo_ready = sem("ehlo_ready")
        edown_ready = sem("edown_ready"); ostaged = sem("ostaged")
        ostored = [sem(f"ostored{r}") for r in range(2)]
        cidx_copied = sem("cidx_copied")
        crows = [sem(f"crows{r}") for r in range(4)]
        cfirst = sem("cfirst"); combined = sem("combined"); out_stored = sem("out_stored")

        def acc_tile(c):
            return acc[:, bass.ds(c * D, D)]

        block = es.enter_context(nc.Block())

        def tiles_at(first, step):
            return [k for k in range(GT) if first + 3 * k == step]

        @block.sync
        def _(sp):
            def load_tile(quad, j, r):
                for q in range(Q):
                    src = [t[bass.ds(quad * Q + q, 1), bass.ds(j * TS, TS), :].rearrange("b t d -> (b t) d")
                           for t in (x, ctx_in)]
                    dst = acc[q * TS:(q + 1) * TS, bass.ds((quad * TPQ + j) * D, D)]
                    sp.dma_start(dst, src[0]).then_inc(in_loaded[r], 16)
                    sp.dma_start(ctxb[r][q * TS:(q + 1) * TS, :], src[1]).then_inc(in_loaded[r], 16)

            def attn_tiles(quad, half, last=False):
                for k in range(GT):
                    c = quad * TPQ + half * GT + k
                    sp.wait_ge(v_turned, c + 1)
                    if not (last and k >= GT - 2):
                        if half * GT + k + 2 < TPQ:
                            load_tile(quad, half * GT + k + 2, k % 2)
                        else:
                            load_tile(quad + 1, half * GT + k + 2 - TPQ, k % 2)
                    sp.wait_ge(xln_ready, c + 1)
                    sp.dma_start(xln_d[bass.ds(c * P, P), :], xln[k % 2]).then_inc(xln_stored[k % 2], 16)

            for r in range(2):
                sp.sem_inc(ostored[r], 16)
            load_tile(0, 0, 0)
            load_tile(0, 1, 1)
            attn_tiles(0, 0)
            with sp.Fori(0, QUADS - 1) as n:
                attn_tiles(n, 1)
                attn_tiles(n + 1, 0)
            attn_tiles(QUADS - 1, 1, last=True)

            sp.wait_ge(slots_sent, 16 * TOPK * TILES)
            sp.dma_start(tokt, slot_tok_d[0:E * CAP, :].rearrange("(a b) o -> a (b o)", b=P)).then_inc(slots_back, 16)

            def load_expert(e, p, i):
                for q in range(WCH):
                    load_chunk(e, p, i, q)

            def load_chunk(e, p, i, q):
                w = WCH * e + q
                r = (p + q) % 2
                if isinstance(e, int) and w < 2:
                    sp.wait_ge(gidx_ready, 1)
                else:
                    sp.wait_ge(ew_lo, w - 1)
                if q < 2 * KT:
                    k, g = q // 2, q % 2
                    src = w_ug[bass.ds(e, 1), k * P:(k + 1) * P, g * I:(g + 1) * I].rearrange("e k c -> (e k) c")
                    sp.dma_start(wst[r][:, 0:I], src).then_inc(ew_in[r], 16)
                else:
                    j = q - 2 * KT
                    src = w_dn[bass.ds(e, 1), j * P:j * P + IM[j], :].rearrange("e k c -> (e k) c")
                    sp.dma_start(wst[r][0:IM[j], :], src).then_inc(ew_in[r], 16)

            def expert(e, p, i, more):
                for j in range(EC):
                    cc = EC * e + j
                    if more:
                        for q in CONV[j]:
                            load_chunk(e + 1, 1 - p, i + p, q)
                    for t in range(2):
                        sp.wait_ge(ostaged, 2 * cc + t + 1)
                        sp.dma_start(slot_out_d[bass.ds((2 * cc + t) * P, P), :], ostage[t]).then_inc(ostored[t], 16)

            load_expert(0, 0, 0)
            with sp.Fori(0, E // 2 - 1) as i:
                expert(2 * i, 0, i, True)
                expert(2 * i + 1, 1, i, True)
            expert(E - 2, 0, E // 2 - 1, True)
            expert(E - 1, 1, E // 2 - 1, False)

            def store_group(quad, half):
                sp.wait_ge(combined, GT * (2 * quad + half + 1))
                for q in range(Q):
                    src = acc[q * TS:(q + 1) * TS, bass.ds((quad * TPQ + half * GT) * D, GT * D)].rearrange(
                        "t (j d) -> t j d", j=GT)
                    dst = out[bass.ds(quad * Q + q, 1), half * GT * TS:(half + 1) * GT * TS, :].rearrange(
                        "b (j t) d -> (b t) j d", j=GT)
                    sp.dma_start(dst, src).then_inc(out_stored, 16)

            with sp.Fori(0, QUADS) as n:
                store_group(n, 0)
                store_group(n, 1)
            sp.wait_ge(out_stored, 16 * GROUPS * Q)
            for r in range(2):
                sp.wait_ge(ostored[r], 16 * (E * EC + 1))
                sp.wait_ge(xln_stored[r], 16 * TILES // 2)

        @block.gpsimd
        def _(pool):
            made_n = [0]

            def chain(ins):
                made_n[0] += 1
                ins.then_inc(pmade, 1)
                pool.wait_ge(pmade, made_n[0])

            chain(pool.memset(ident[:, :], 0.0))
            chain(pool.affine_select(out=ident[:, :], in_=ident[:, :], compare_op=ALU.not_equal, fill=1.0, base=0,
                                     pattern=[[-1, P]], channel_multiplier=1))
            chain(pool.memset(prefw, 1.0))
            for m in (0, 2):
                chain(pool.affine_select(out=prefw[:, m], in_=prefw[:, m], compare_op=ALU.is_ge, fill=0.0, base=0,
                                         pattern=[[-TS, Q], [0, TS]], channel_multiplier=1))
                chain(pool.affine_select(out=prefw[:, m], in_=prefw[:, m], compare_op=ALU.is_ge, fill=0.0,
                                         base=TS - 1, pattern=[[TS, Q], [0, TS]], channel_multiplier=-1))
            chain(pool.affine_select(out=prefw[:, 1], in_=prefw[:, 1], compare_op=ALU.is_ge, fill=0.0, base=-1,
                                     pattern=[[TS, Q], [0, TS]], channel_multiplier=-1))
            chain(pool.affine_select(out=prefw[:, 2], in_=prefw[:, 2], compare_op=ALU.is_ge, fill=0.0, base=-1,
                                     pattern=[[TS, Q], [1, TS]], channel_multiplier=-1))
            chain(pool.tensor_copy(pref[:, :, :].rearrange("p m (q r) -> p m q r", q=Q), prefw))
            chain(pool.iota(iotae[:, :], pattern=[[1, E]], base=0, channel_multiplier=0,
                            allow_small_or_imprecise_dtypes=True))
            chain(pool.iota(rowid[:, :], pattern=[[P, TILES]], base=0, channel_multiplier=1,
                            allow_small_or_imprecise_dtypes=True))
            chain(pool.memset(mhalf[:, :], -0.5))
            pool.wait_ge(tabs, TABS)

            def wait_alone(s, v):
                pool.wait_ge(s, v)
                pool.sem_inc(pool_waits, 1)

            def inv_std(n, done_v, done_r, c):
                pool.wait_ge(done_v, c + 1)
                pool.tensor_tensor(rstd[:, n:n + 1], ve[:, n:n + 1], mhalf[:, :], ALU.pow).then_inc(done_r, 1)

            def products(c, k, first):
                ekv = ek.rearrange("p (h t) -> p h t", h=HB)
                vv = vT.rearrange("p (h t) -> p h t", h=HB)

                def tab(n):
                    return e12[:, n, :].unsqueeze(2).to_broadcast([P, HB, TS])
                pool.wait_ge(ek_ready, c + 1)
                if not (first and k == 0):
                    pool.wait_ge(scanned, c)
                pool.tensor_tensor(scan_in[:, 1, :, 1:SEG], ekv, tab(0), ALU.mult).then_inc(pw, 1)
                pool.wait_ge(pw, 2 * c + 1)
                pool.wait_ge(v_turned, c + 1)
                pool.tensor_tensor(scan_in[:, 0, :, 1:SEG], scan_in[:, 1, :, 1:SEG], vv, ALU.mult).then_inc(scan_in_ready, 1)
                if not (first and k == 0):
                    pool.wait_ge(y_turned, c)
                pool.tensor_tensor(nd[:, 1], ekv, tab(1), ALU.mult).then_inc(pw, 1)
                pool.wait_ge(pw, 2 * c + 2)
                pool.tensor_tensor(nd[:, 0], nd[:, 1], vv, ALU.mult).then_inc(nd_ready, 1)

            def attn_group(g, first=False):
                for s in range(SLOTS):
                    for k in tiles_at(0, s):
                        inv_std(0, var1, rstd1, GT * g + k)
                    for k in tiles_at(3, s):
                        inv_std(1, var2, rstd2, GT * g + k)
                    for k in tiles_at(1, s):
                        products(GT * g + k, k, first)

            attn_group(0, first=True)
            with pool.Fori(0, QUADS - 1) as n:
                attn_group(2 * n + 1)
                attn_group(2 * n + 2)
            attn_group(GROUPS - 1)

            pool.wait_ge(routed, 1)
            pool.memset(zslot, 0.0).then_inc(zeros_made, 1)
            pool.wait_ge(zeros_made, 1)
            pool.dma_start(slot_tok_d[0:E * CAP, :].rearrange("(a b) o -> a (b o)", b=P), zslot).then_inc(slots_zeroed, 16)
            pool.wait_ge(slots_zeroed, 16)
            with pool.Fori(0, GROUPS) as n:
                pool.tensor_copy(sidx[:, :], sslot[:, bass.ds(2 * GT * n, 2 * GT)]).then_inc(idx_copied, 1)
                pool.tensor_copy(stok[:, :], rowid[:, bass.ds(GT * n, GT)]).then_inc(idx_copied, 1)
                wait_alone(idx_copied, 2 * n + 2)
                for t in range(GT):
                    for k in range(TOPK):
                        pool.indirect_dma_start(
                            out=slot_tok_d, out_offset=bass.IndirectOffsetOnAxis(ap=sidx[:, 2 * t + k:2 * t + k + 1], axis=0),
                            in_=stok[:, t:t + 1], in_offset=None).then_inc(slots_sent, 16)
                pool.wait_ge(slots_sent, 16 * 2 * GT * n + 16 * 2 * GT)

            pool.wait_ge(gidx_ready, 1)
            pool.wait_ge(hlo_ready, JT * GROUPS)
            for r in range(2):
                pool.wait_ge(xln_stored[r], 16 * TILES // 2)

            def gather_expert(e, p, first):
                pool.tensor_copy(eidx[:, p, :], gidx[:, bass.ds(ET * e, ET)]).then_inc(eidx_ready, 1)
                wait_alone(eidx_ready, e + 1)
                for s in range(ET):
                    if not (first and s < 2):
                        wait_alone(xg_turned, ET * e + s - 1)
                    pool.indirect_dma_start(
                        out=xg[s % 2], out_offset=None, in_=xln_d,
                        in_offset=bass.IndirectOffsetOnAxis(ap=eidx[:, p, s:s + 1], axis=0)).then_inc(gathered[s % 2], 16)

            gather_expert(0, 0, True)
            gather_expert(1, 1, False)
            with pool.Fori(1, E // 2) as i:
                gather_expert(2 * i, 0, False)
                gather_expert(2 * i + 1, 1, False)

            for r in range(2):
                pool.wait_ge(ostored[r], 16 * (E * EC + 1))
            pool.wait_ge(eup_ready, IT * E * EC)
            def gather_rows(c, t):
                pool.tensor_copy(sidx[:, 2 * t:2 * t + 2], cslot[:, bass.ds(2 * c, 2)]).then_inc(cidx_copied, 1)
                wait_alone(cidx_copied, c + 1)
                for k in range(TOPK):
                    pool.indirect_dma_start(
                        out=cg[t][:, k, :], out_offset=None, in_=slot_out_d,
                        in_offset=bass.IndirectOffsetOnAxis(ap=sidx[:, 2 * t + k:2 * t + k + 1], axis=0)).then_inc(crows[t], 16)

            for t in range(GT):
                gather_rows(t, t)
            with pool.Fori(1, GROUPS) as n:
                for t in range(GT):
                    pool.wait_ge(combined, GT * n + t + 1 - GT)
                    gather_rows(GT * n + t, t)

        @block.scalar
        def _(act):
            act.dma_start(gates[:, 0:1], g_x.partition_broadcast(P)).then_inc(const_in, 16)
            act.dma_start(gates[:, 1:2], g_f.partition_broadcast(P)).then_inc(const_in, 16)
            act.wait_ge(tab_zeroed, 1)
            for q in range(Q):
                for n, t in enumerate((t_first, t_decay)):
                    act.dma_start(tab_rows[q * 32:q * 32 + HB, n, :], t.rearrange("(h l) -> h l", l=32)).then_inc(tab_in, 16)
            act.dma_start(rt_f[:, :, :], router.rearrange("(k p) e -> p k e", p=P)).then_inc(const_in, 16)
            ug_v = s_ug.rearrange("(k p) (g m c) -> p g m k c", p=P, g=2, m=JT)
            dn_v = s_dn.rearrange("(j p) c -> p j c", p=P)

            def load_u(m):
                for g in range(2):
                    act.dma_start(sst_u[:, m % 4, g], ug_v[:, g, m]).then_inc(wu_in[m % 4], 16)

            def load_d(j):
                act.dma_start(sst_d[:, j % 3], dn_v[:, j]).then_inc(wd_in[j % 3], 16)

            for m in range(4):
                load_u(m)
            for j in range(3):
                load_d(j)

            act.wait_ge(const_in, 16 * 3)
            act.activation(gates[:, 2:4], gates[:, 0:2], ACT.Tanh).then_inc(exps, 1)
            act.wait_ge(tab_turned, 2)
            act.activation(decay[:, :, 1], tab_cols[:, 1, 0:HB], ACT.Exp).then_inc(exps, 1)
            act.wait_ge(exps, 2)
            act.activation(decay[:, :, 2], decay[:, :, 1], ACT.Exp, scale=-1.0).then_inc(exps, 1)
            act.wait_ge(consts, 2)
            act.activation(e12[:, :, :], e12[:, :, :], ACT.Exp).then_inc(exps, 1)
            act.activation(rt_w[:, 0], rt_f[:, :, :], ACT.Copy, scale=WS).then_inc(rhi, 1)

            def split_hi(m):
                act.wait_ge(wu_in[m % 4], 32 * (m // 4 + 1))
                act.activation(sU[:, m, :, 0], sst_u[:, m % 4], ACT.Copy, scale=WS).then_inc(wu_hi, 1)
                act.wait_ge(wd_in[m % 3], 16 * (m // 3 + 1))
                act.activation(sD[:, m, 0], sst_d[:, m % 3], ACT.Copy, scale=WS).then_inc(wd_hi, 1)
                if m >= 1 and m + 3 < JT:
                    act.wait_ge(wu_lo, m)
                    load_u(m + 3)
                if m >= 1 and m + 2 < JT:
                    act.wait_ge(wd_lo, m)
                    load_d(m + 2)

            def exp_k(c):
                act.wait_ge(k_turned, c + 1)
                act.activation(ek, ek, ACT.Exp).then_inc(ek_ready, 1)

            def x_hi(g, k, first, par):
                c = GT * g + k
                act.wait_ge(x_turned, c + 1)
                act.activation(xT[:, par, 0, :, k * P:(k + 1) * P], PT[:, :].rearrange("p (k t) -> p k t", k=KT),
                               ACT.Copy).then_inc(xhi_ready, 1)

            def shared_hidden(g, gpar, m):
                n = JT * g + m
                r = (gpar + m) % 2
                act.wait_ge(up_ready, n + 1)
                if m >= 2:
                    act.wait_ge(hlo_ready, n - 1)
                act.activation(srng[:, r, :], PU[r][0][:, :], ACT.Silu, scale=1.0 / WS).then_inc(silu_done, 1)
                act.wait_ge(h_ready, n + 1)
                act.activation(hh[:, m, 0, :], srng[:, r, :], ACT.Copy).then_inc(hhi_ready, 1)

            def group(gs, ga, gpar, first=False):
                for s in range(SLOTS):
                    if ga is not None:
                        for k in tiles_at(1, s):
                            exp_k(GT * ga + k)
                        for k in tiles_at(5, s):
                            x_hi(ga, k, first, 1 - gpar)
                    if gs is None:
                        if s < JT:
                            split_hi(s)
                    elif s < JT:
                        shared_hidden(gs, gpar, s)

            group(None, 0, 1, first=True)
            with act.Fori(0, QUADS - 1) as n:
                group(2 * n, 2 * n + 1, 0)
                group(2 * n + 1, 2 * n + 2, 1)
            group(GROUPS - 2, GROUPS - 1, 0)
            act.wait_ge(rsteps, R_EXP)
            act.activation(wtmp[:, 1], wtmp[:, 0], ACT.Exp).then_inc(exps, 1)
            group(GROUPS - 1, None, 1)

            def weights_hi(e, p, q, half):
                w = WCH * e + q
                r = (p + q) % 2
                act.wait_ge(ew_in[r], 16 * (WCH * half + (WCH * p + q) // 2 + 1))
                if q < 2 * KT:
                    act.activation(eU[p][:, q % 2, 0, q // 2], wst[r][:, 0:I], ACT.Copy, scale=WS).then_inc(ew_hi, 1)
                else:
                    j = q - 2 * KT
                    act.activation(eD[p][0:IM[j], j, 0], wst[r][0:IM[j], :], ACT.Copy, scale=WS).then_inc(ew_hi, 1)

            def gather_hi(e, p, j):
                cc = EC * e + j
                for t in range(2):
                    act.wait_ge(xg_turned, 2 * cc + t + 1)
                    if not (isinstance(e, int) and cc < 2):
                        act.wait_ge(eup_ready, IT * (cc - 1))
                    T = (PT, PR)[t]
                    act.activation(xgT[:, (p + j) % 2, 0, :, t * P:(t + 1) * P],
                                   T[:, :].rearrange("p (k t) -> p k t", k=KT), ACT.Copy).then_inc(xg_hi, 1)

            def expert_hidden(e, p, j, m):
                cc = EC * e + j
                n = IT * cc + m
                r = (p + j + m) % 2
                M = IM[m]
                act.wait_ge(eup_ready, n + 1)
                if not (isinstance(e, int) and n < 2):
                    act.wait_ge(ehlo_ready, n - 1)
                act.activation(esr[r][0:M, :], PU[r][0][0:M, 0:CH], ACT.Silu, scale=1.0 / WS).then_inc(esilu_done, 1)
                act.wait_ge(eh_ready, n + 1)
                act.activation(eh[0:M, (p + j) % 2, m, 0, :], esr[r][0:M, :], ACT.Copy).then_inc(ehhi_ready, 1)

            def stage_out(e, p, j):
                cc = EC * e + j
                for t in range(2):
                    act.wait_ge(edown_ready, 2 * cc + t + 1)
                    act.wait_ge(ostored[t], 16 * cc + 16)
                    act.activation(ostage[t], PD[t][:, :], ACT.Copy, scale=1.0 / (WS * HS)).then_inc(ostaged, 1)

            def expert(e, p, half, last=False):
                for j in range(EC):
                    if not last:
                        for q in CONV[j]:
                            weights_hi(e + 1, 1 - p, q, half + p)
                    if j + 1 < EC:
                        for m in range(IT):
                            expert_hidden(e, p, j + 1, m)
                    elif not last:
                        for m in range(IT):
                            expert_hidden(e + 1, 1 - p, 0, m)
                    if j + 2 < EC:
                        gather_hi(e, p, j + 2)
                    elif not last:
                        gather_hi(e + 1, 1 - p, j + 2 - EC)
                    stage_out(e, p, j)

            act.wait_ge(down_added, TILES)
            for q in range(WCH):
                weights_hi(0, 0, q, 0)
            gather_hi(0, 0, 0)
            for m in range(IT):
                expert_hidden(0, 0, 0, m)
            gather_hi(0, 0, 1)
            with act.Fori(0, E // 2 - 1) as i:
                expert(2 * i, 0, i)
                expert(2 * i + 1, 1, i)
            expert(E - 2, 0, E // 2 - 1)
            expert(E - 1, 1, E // 2 - 1, last=True)

        @block.tensor
        def _(pe):
            def turn_tile(c, k, first):
                pe.wait_ge(xln_ready, c + 1)
                if not (first and k == 0):
                    pe.wait_ge(xlo_ready, c)
                for kt in range(KT):
                    mm = pe.transpose(PT[:, kt * P:(kt + 1) * P], xln[k % 2][:, kt * P:(kt + 1) * P], ident[:, :])
                mm.then_inc(x_turned, 1)

            def logits(c, k, first, par):
                pe.wait_ge(xlo_ready, c + 1)
                if not (first and k == 0):
                    pe.wait_ge(logits_taken, c)
                for hl in range(2):
                    for kt in range(KT):
                        mm = pe.matmul(PR[:, 0:2 * E], xT[:, par, hl, kt, k * P:(k + 1) * P], rt_w[:, :, kt, :],
                                       start=(hl == 0 and kt == 0), stop=(hl == 1 and kt == KT - 1))
                mm.then_inc(logits_ready, 1)

            def up_pair(g, gpar, m):
                n = JT * g + m
                r = (gpar + m) % 2
                if m >= 2:
                    pe.wait_ge(h_ready, n - 1)
                for gu in range(2):
                    for kt in range(KT):
                        for a, b in ((0, 0), (0, 1), (1, 0)):
                            mm = pe.matmul(PU[r][gu][:, :], sU[:, m, gu, a, kt, :], xT[:, gpar, b, kt, :],
                                           start=(kt == 0 and a + b == 0), stop=(kt == KT - 1 and a == 1))
                mm.then_inc(up_ready, 1)

            def down_tile(g, t):
                n = GT * g + t
                if t >= 2:
                    pe.wait_ge(down_added, n - 1)
                for j in range(JT):
                    if t == 0:
                        pe.wait_ge(hlo_ready, JT * g + j + 1)
                    for a, b in ((0, 0), (0, 1), (1, 0)):
                        mm = pe.matmul(PD[t % 2][:, :], hh[:, j, a, t * P:(t + 1) * P], sD[:, j, b, :],
                                       start=(j == 0 and a + b == 0), stop=(j == JT - 1 and a == 1))
                mm.then_inc(down_ready, 1)

            def group(gs, ga, gpar, first=False):
                if gs is not None:
                    pe.wait_ge(xlo_ready, GT * (gs + 1))
                for s in range(SLOTS):
                    if ga is not None:
                        for k in tiles_at(5, s):
                            turn_tile(GT * ga + k, k, first)
                        for k in tiles_at(6, s):
                            logits(GT * ga + k, k, first, 1 - gpar)
                    if gs is not None:
                        if s < JT:
                            up_pair(gs, gpar, s)
                        else:
                            down_tile(gs, s - JT)
                if ga is not None:
                    logits(GT * ga + GT - 1, GT - 1, first, 1 - gpar)

            pe.wait_ge(pmade, PMADE)
            pe.wait_ge(rlo, 1)
            group(None, 0, 1, first=True)
            pe.wait_ge(wu_lo, JT)
            pe.wait_ge(wd_lo, JT)
            with pe.Fori(0, QUADS - 1) as n:
                group(2 * n, 2 * n + 1, 0)
                group(2 * n + 1, 2 * n + 2, 1)
            group(GROUPS - 2, GROUPS - 1, 0)

            pe.wait_ge(rsteps, R_PREF)
            pe.wait_ge(logits_taken, TILES)
            for m, rhs in enumerate((ohx, ohtot, ohs, ohrun)):
                mm = pe.matmul(PR[:, 0:TILES * E], pref[:, m, :], rhs, start=(m == 0), stop=(m == 3))
            mm.then_inc(pos_ready, 1)
            group(GROUPS - 1, None, 1)

            def turn_slots(e, p, j):
                cc = EC * e + j
                for t in range(2):
                    s = 2 * j + t
                    pe.wait_ge(gathered[t], 16 * cc + 16)
                    if not isinstance(e, int) or cc > 0:
                        pe.wait_ge(xg_lo, 2 * cc)
                    T = (PT, PR)[t]
                    for kt in range(KT):
                        mm = pe.transpose(T[:, kt * P:(kt + 1) * P], xg[s % 2][:, kt * P:(kt + 1) * P], ident[:, :])
                    mm.then_inc(xg_turned, 1)

            def up_chunk(e, p, j):
                cc = EC * e + j
                if j == 0:
                    pe.wait_ge(ew_lo, WCH * (e + 1))
                pe.wait_ge(xg_lo, 2 * cc + 2)
                for m in range(IT):
                    n = IT * cc + m
                    r = (p + j + m) % 2
                    M = IM[m]
                    if not (isinstance(e, int) and n < 2):
                        pe.wait_ge(eh_ready, n - 1)
                    for gu in range(2):
                        for kt in range(KT):
                            for a, b in ((0, 0), (0, 1), (1, 0)):
                                mm = pe.matmul(PU[r][gu][0:M, 0:CH], eU[p][:, gu, a, kt, m * P:m * P + M],
                                               xgT[:, (p + j) % 2, b, kt, :],
                                               start=(kt == 0 and a + b == 0), stop=(kt == KT - 1 and a == 1))
                    mm.then_inc(eup_ready, 1)

            def down_chunk(e, p, j):
                cc = EC * e + j
                pe.wait_ge(ehlo_ready, IT * (cc + 1))
                for t in range(2):
                    if j > 0:
                        pe.wait_ge(ostaged, 2 * cc)
                    for m in range(IT):
                        M = IM[m]
                        for a, b in ((0, 0), (0, 1), (1, 0)):
                            mm = pe.matmul(PD[t][:, :], eh[0:M, (p + j) % 2, m, a, t * P:(t + 1) * P],
                                           eD[p][0:M, m, b, :],
                                           start=(m == 0 and a + b == 0), stop=(m == IT - 1 and a == 1))
                    mm.then_inc(edown_ready, 1)

            def expert(e, p, last=False):
                for j in range(EC):
                    if j + 1 < EC:
                        up_chunk(e, p, j + 1)
                    elif not last:
                        up_chunk(e + 1, 1 - p, 0)
                    if j + 2 < EC:
                        turn_slots(e, p, j + 2)
                    elif not last:
                        turn_slots(e + 1, 1 - p, j + 2 - EC)
                    down_chunk(e, p, j)

            pe.wait_ge(slots_back, 16)
            pe.wait_ge(rsteps, R_POS)
            pe.transpose(PR[:, 0:E * ET], tokt, ident[0:E * ET, 0:E * ET]).then_inc(slots_turned, 1)
            pe.wait_ge(gidx_ready, 1)
            pe.wait_ge(down_added, TILES)
            turn_slots(0, 0, 0)
            up_chunk(0, 0, 0)
            turn_slots(0, 0, 1)
            with pe.Fori(0, E // 2 - 1) as i:
                expert(2 * i, 0)
                expert(2 * i + 1, 1)
            expert(E - 2, 0)
            expert(E - 1, 1, last=True)

        @block.vector
        def _(dve):
            ntab = [0]

            def tab_step(ins):
                ntab[0] += 1
                ins.then_inc(tabs, 1)
                dve.wait_ge(tabs, ntab[0])

            dve.memset(tab_rows, 0.0).then_inc(tab_zeroed, 1)
            dve.wait_ge(tab_in, 16 * 2 * Q)
            for n in range(2):
                dve.transpose(tab_cols[:, n], tab_rows[:, n]).then_inc(tab_turned, 1)
            dve.wait_ge(exps, 3)
            tab_step(dve.tensor_copy(decay[:, :, 3:SEG], decay[:, :, 2].unsqueeze(2).to_broadcast([P, HB, SEG - 3])))
            tab_step(dve.tensor_copy(decay[:, :, 1], decay[:, :, 2]))
            tab_step(dve.memset(decay[:, :, 0], 0.0))
            dve.tensor_scalar(e12[:, 1, :], tab_cols[:, 0, 0:HB], 0.0, None, ALU.min).then_inc(consts, 1)
            dve.wait_ge(consts, 1)
            dve.tensor_scalar(e12[:, 0, :], tab_cols[:, 0, 0:HB], 0.0, -1.0, ALU.max, ALU.mult).then_inc(consts, 1)
            dve.wait_ge(exps, 4)
            tab_step(dve.tensor_scalar(gates[:, 0:1], gates[:, 3:4], 1.0 / (WS * HS), None, ALU.mult))
            dve.wait_ge(rhi, 1)
            dve.scalar_tensor_tensor(out=rt_w[:, 1], in0=rt_f[:, :, :], scalar=WS, in1=rt_w[:, 0],
                                     op0=ALU.mult, op1=ALU.subtract).then_inc(rlo, 1)
            tab_step(dve.memset(lt[:, :], 0.0))
            tab_step(dve.memset(topv[:, :], 0.0))
            assert ntab[0] == TABS

            def wait_alone(s, v):
                dve.wait_ge(s, v)
                dve.sem_inc(dve_waits, 1)

            def stats(c, n, bn_done, var_done):
                dve.bn_stats(bn[:, n, :], acc_tile(c)).then_inc(bn_done, 1)
                wait_alone(bn_done, 2 * c + 1)
                dve.bn_aggr(mv[:, n, :], bn[:, n, :]).then_inc(bn_done, 1)
                dve.wait_ge(bn_done, 2 * c + 2)
                dve.tensor_scalar(ve[:, n:n + 1], mv[:, n, 1:2], EPS, None, ALU.add).then_inc(var_done, 1)

            def stage_b(c, k):
                dve.wait_ge(rstd1, c + 1)
                dve.tensor_scalar(kbuf, acc_tile(c), mv[:, 0, 0:1], rstd[:, 0:1], ALU.subtract, ALU.mult).then_inc(k_norm, 1)
                dve.wait_ge(k_norm, c + 1)
                dve.transpose(ek, kbuf).then_inc(k_turned, 1)
                dve.transpose(vT, ctxb[k % 2]).then_inc(v_turned, 1)

            def stage_c(c, k, start, first):
                if start:
                    dve.memset(scan_in[:, :, :, 0], 0.0).then_inc(carried, 1)
                else:
                    dve.wait_ge(scanned, c)
                    dve.tensor_copy(scan_in[:, :, :, 0], scan_out[:, :, :, TS]).then_inc(carried, 1)
                dve.wait_ge(carried, c + 1)
                dve.wait_ge(scan_in_ready, c + 1)
                for n in range(2):
                    ins = dve.tensor_tensor_scan(scan_out[:, n].rearrange("p h s -> p (h s)"),
                                                 decay.rearrange("p h s -> p (h s)"),
                                                 scan_in[:, n].rearrange("p h s -> p (h s)"), 0.0, ALU.mult, ALU.add)
                ins.then_inc(scanned, 1)
                dve.wait_ge(scanned, c + 1)
                dve.wait_ge(nd_ready, c + 1)
                dve.tensor_tensor(nd, nd, scan_out[:, :, :, 0:TS], ALU.add).then_inc(summed, 1)

            def stage_d(c, k, start):
                rcp = ek
                wait_alone(summed, c + 1)
                dve.reciprocal(rcp, nd[:, 1].rearrange("p h t -> p (h t)")).then_inc(rcp_done, 1)
                dve.wait_ge(rcp_done, c + 1)
                y = nd[:, 0]
                dve.tensor_tensor(y, y, rcp.rearrange("p (h t) -> p h t", h=HB), ALU.mult).then_inc(y_done, 1)
                if start:
                    dve.wait_ge(y_done, 2 * c + 1)
                    dve.tensor_copy(nd[:, 0, :, 0], vT.rearrange("p (h t) -> p h t", h=HB)[:, :, 0]).then_inc(y_done, 1)
                else:
                    dve.sem_inc(y_done, 1)
                dve.wait_ge(y_done, 2 * c + 2)
                dve.transpose(kbuf, nd[:, 0].rearrange("p h t -> p (h t)")).then_inc(y_turned, 1)
                dve.wait_ge(y_turned, c + 1)
                dve.scalar_tensor_tensor(out=acc_tile(c), in0=kbuf, scalar=gates[:, 2:3], in1=acc_tile(c),
                                         op0=ALU.mult, op1=ALU.add).then_inc(x2_done, 1)
                wait_alone(x2_done, c + 1)
                stats(c, 1, bn2, var2)

            def stage_f(c, k, par):
                dve.wait_ge(xhi_ready, c + 1)
                dve.tensor_tensor(xT[:, par, 1, :, k * P:(k + 1) * P], PT[:, :].rearrange("p (k t) -> p k t", k=KT),
                                  xT[:, par, 0, :, k * P:(k + 1) * P], ALU.subtract).then_inc(xlo_ready, 1)

            def stage_r(c):
                dve.wait_ge(logits_ready, c + 1)
                dve.tensor_reduce(lt[:, :], PR[:, 0:2 * E].rearrange("p (n e) -> p e n", n=2), AX.X, ALU.add).then_inc(logits_taken, 1)
                wait_alone(logits_taken, c + 1)
                dve.max(top8[:, :], lt[:, :]).then_inc(top_steps, 1)
                wait_alone(top_steps, 4 * c + 1)
                dve.max_index(top8i[:, :], top8[:, :], lt[:, :]).then_inc(top_steps, 1)
                dve.wait_ge(top_steps, 4 * c + 2)
                dve.tensor_copy(topv[:, bass.ds(2 * c, 2)], top8[:, 0:2]).then_inc(top_steps, 1)
                dve.tensor_copy(topi[:, bass.ds(2 * c, 2)], top8i[:, 0:2]).then_inc(top_steps, 1)

            def split_lo(m):
                dve.wait_ge(wu_hi, m + 1)
                dve.scalar_tensor_tensor(out=sU[:, m, :, 1], in0=sst_u[:, m % 4], scalar=WS, in1=sU[:, m, :, 0],
                                         op0=ALU.mult, op1=ALU.subtract).then_inc(wu_lo, 1)
                dve.wait_ge(wd_hi, m + 1)
                dve.scalar_tensor_tensor(out=sD[:, m, 1], in0=sst_d[:, m % 3], scalar=WS, in1=sD[:, m, 0],
                                         op0=ALU.mult, op1=ALU.subtract).then_inc(wd_lo, 1)

            def shared_hidden(g, gpar, m):
                n = JT * g + m
                r = (gpar + m) % 2
                dve.wait_ge(silu_done, n + 1)
                dve.scalar_tensor_tensor(out=srng[:, r, :], in0=PU[r][1][:, :], scalar=HS / WS, in1=srng[:, r, :],
                                         op0=ALU.mult, op1=ALU.mult).then_inc(h_ready, 1)
                dve.wait_ge(hhi_ready, n + 1)
                dve.tensor_tensor(hh[:, m, 1, :], srng[:, r, :], hh[:, m, 0, :], ALU.subtract).then_inc(hlo_ready, 1)

            def add_down(g, t):
                n = GT * g + t
                dve.wait_ge(down_ready, n + 1)
                dve.scalar_tensor_tensor(out=acc_tile(n), in0=PD[t % 2][:, :], scalar=gates[:, 0:1], in1=acc_tile(n),
                                         op0=ALU.mult, op1=ALU.add).then_inc(down_added, 1)

            def group(gs, ga, gpar, first=False, second=False):
                par = 1 - gpar
                start = par == 0
                for s in range(SLOTS):
                    if ga is not None:
                        for k in tiles_at(1, s):
                            stage_b(GT * ga + k, k)
                        for k in tiles_at(4, s):
                            stage_e(ga, k, first)
                        for k in tiles_at(0, s):
                            stage_a(ga, k)
                        for k in tiles_at(3, s):
                            stage_d(GT * ga + k, k, start and k == 0)
                        for k in tiles_at(2, s):
                            stage_c(GT * ga + k, k, start and k == 0, first)
                        for k in tiles_at(5, s):
                            stage_f(GT * ga + k, k, par)
                        for k in tiles_at(6, s):
                            stage_r(GT * ga + k)
                    if gs is None:
                        if s < JT:
                            split_lo(s)
                    elif s < JT:
                        shared_hidden(gs, gpar, s)
                    else:
                        add_down(gs, s - JT)
                if ga is not None:
                    stage_r(GT * ga + GT - 1)

            def stage_a(g, k):
                wait_alone(in_loaded[k % 2], 128 * (2 * g + k // 2 + 1))
                stats(GT * g + k, 0, bn1, var1)

            def stage_e(g, k, first):
                c = GT * g + k
                dve.wait_ge(rstd2, c + 1)
                if not (first and k < 2):
                    dve.wait_ge(xln_stored[k % 2], 16 * (2 * g + k // 2))
                    dve.wait_ge(x_turned, c - 1)
                dve.tensor_scalar(xln[k % 2], acc_tile(c), mv[:, 1, 0:1], rstd[:, 1:2],
                                  ALU.subtract, ALU.mult).then_inc(xln_ready, 1)

            group(None, 0, 1, first=True)
            with dve.Fori(0, QUADS - 1) as n:
                group(2 * n, 2 * n + 1, 0)
                group(2 * n + 1, 2 * n + 2, 1)
            group(GROUPS - 2, GROUPS - 1, 0)

            nr = [0]

            def step(ins):
                nr[0] += 1
                ins.then_inc(rsteps, 1)
                dve.wait_ge(rsteps, nr[0])

            dve.wait_ge(top_steps, 4 * TILES)
            tv = topv[:, :].rearrange("p (t n) -> p n t", n=2)
            ti = topi[:, :].rearrange("p (t n) -> p n t", n=2)
            step(dve.tensor_tensor(wtmp[:, 0], tv[:, 1], tv[:, 0], ALU.subtract))
            step(dve.tensor_scalar(wtmp[:, 0], wtmp[:, 0], 1.0 / WS, None, ALU.mult))
            assert nr[0] == R_EXP
            for k in range(TOPK):
                step(dve.tensor_tensor(oh[:, k], ti[:, k].unsqueeze(2).to_broadcast([P, TILES, E]),
                                       iotae[:, :].unsqueeze(1).to_broadcast([P, TILES, E]), ALU.is_equal))
            o4 = ohs.rearrange("p (b j e) -> p b j e", b=QUADS, j=TPQ)
            x4 = ohx.rearrange("p (b j e) -> p b j e", b=QUADS, j=TPQ)
            step(dve.tensor_tensor(ohs.rearrange("p (t e) -> p t e", e=E), oh[:, 0], oh[:, 1], ALU.add))
            step(dve.memset(x4[:, :, 0], 0.0))
            for j in range(1, TPQ):
                step(dve.tensor_tensor(x4[:, :, j], x4[:, :, j - 1], o4[:, :, j - 1], ALU.add))
            step(dve.tensor_tensor(tot, x4[:, :, TPQ - 1], o4[:, :, TPQ - 1], ALU.add))
            step(dve.memset(run[:, 0], 0.0))
            for b in range(1, QUADS):
                step(dve.tensor_tensor(run[:, b], run[:, b - 1], tot[:, b - 1], ALU.add))
            for dst, src in ((ohtot, tot), (ohrun, run)):
                step(dve.tensor_copy(dst.rearrange("p (b j e) -> p b j e", b=QUADS, j=TPQ),
                                     src.unsqueeze(2).to_broadcast([P, QUADS, TPQ, E])))
            assert nr[0] == R_PREF, nr[0]
            dve.wait_ge(pos_ready, 1)
            step(dve.tensor_copy(pos, PR[:, 0:TILES * E].rearrange("p (t e) -> p t e", e=E)))
            assert nr[0] == R_POS
            for k in range(TOPK):
                step(dve.tensor_tensor(sprod[:, k], oh[:, k], pos, ALU.mult))
            step(dve.tensor_reduce(posk, sprod, AX.X, ALU.add))
            step(dve.tensor_scalar(valid, posk, float(CAP), None, ALU.is_lt))
            step(dve.tensor_scalar(posk, posk, float(CAP - 1), None, ALU.min))
            step(dve.scalar_tensor_tensor(out=slot, in0=ti, scalar=float(CAP), in1=posk, op0=ALU.mult, op1=ALU.add))
            step(dve.tensor_copy(cslot[:, :].rearrange("p (t n) -> p n t", n=2), slot))
            for k in range(TOPK):
                step(dve.tensor_scalar(trash[:, k], rowid[:, :], float(TRASH + NTOK * k), None, ALU.add))
            step(dve.tensor_tensor(slot, slot, trash, ALU.subtract))
            step(dve.tensor_tensor(slot, slot, valid, ALU.mult))
            step(dve.tensor_tensor(slot, slot, trash, ALU.add))
            dve.tensor_copy(sslot[:, :].rearrange("p (t n) -> p n t", n=2), slot).then_inc(routed, 1)
            dve.wait_ge(exps, 5)
            step(dve.tensor_scalar(wtmp[:, 0], wtmp[:, 1], 1.0, None, ALU.add))
            step(dve.reciprocal(wcomb[:, 0, :], wtmp[:, 0]))
            step(dve.tensor_tensor(wcomb[:, 1, :], wcomb[:, 0, :], wtmp[:, 1], ALU.mult))
            step(dve.scalar_tensor_tensor(out=wcomb[:, :, :], in0=wcomb[:, :, :], scalar=gates[:, 3:4], in1=valid,
                                          op0=ALU.mult, op1=ALU.mult))
            group(GROUPS - 1, None, 1)

            dve.wait_ge(slots_turned, 1)
            dve.tensor_copy(gidx[:, :], PR[:, 0:E * ET]).then_inc(gidx_ready, 1)

            def weights_lo(e, p, q):
                w = WCH * e + q
                r = (p + q) % 2
                dve.wait_ge(ew_hi, w + 1)
                if q < 2 * KT:
                    dve.scalar_tensor_tensor(out=eU[p][:, q % 2, 1, q // 2], in0=wst[r][:, 0:I], scalar=WS,
                                             in1=eU[p][:, q % 2, 0, q // 2], op0=ALU.mult, op1=ALU.subtract).then_inc(ew_lo, 1)
                else:
                    j = q - 2 * KT
                    dve.scalar_tensor_tensor(out=eD[p][0:IM[j], j, 1], in0=wst[r][0:IM[j], :], scalar=WS,
                                             in1=eD[p][0:IM[j], j, 0], op0=ALU.mult, op1=ALU.subtract).then_inc(ew_lo, 1)

            def gather_lo(e, p, j):
                for t in range(2):
                    dve.wait_ge(xg_hi, 2 * (EC * e + j) + t + 1)
                    T = (PT, PR)[t]
                    dve.tensor_tensor(xgT[:, (p + j) % 2, 1, :, t * P:(t + 1) * P],
                                      T[:, :].rearrange("p (k t) -> p k t", k=KT),
                                      xgT[:, (p + j) % 2, 0, :, t * P:(t + 1) * P], ALU.subtract).then_inc(xg_lo, 1)

            def expert_hidden(e, p, j, m):
                n = IT * (EC * e + j) + m
                r = (p + j + m) % 2
                M = IM[m]
                dve.wait_ge(esilu_done, n + 1)
                dve.scalar_tensor_tensor(out=esr[r][0:M, :], in0=PU[r][1][0:M, 0:CH], scalar=HS / WS,
                                         in1=esr[r][0:M, :], op0=ALU.mult, op1=ALU.mult).then_inc(eh_ready, 1)
                dve.wait_ge(ehhi_ready, n + 1)
                dve.tensor_tensor(eh[0:M, (p + j) % 2, m, 1, :], esr[r][0:M, :], eh[0:M, (p + j) % 2, m, 0, :],
                                  ALU.subtract).then_inc(ehlo_ready, 1)

            def expert(e, p, last=False):
                for j in range(EC):
                    if not last:
                        for q in CONV[j]:
                            weights_lo(e + 1, 1 - p, q)
                    if j + 1 < EC:
                        for m in range(IT):
                            expert_hidden(e, p, j + 1, m)
                    elif not last:
                        for m in range(IT):
                            expert_hidden(e + 1, 1 - p, 0, m)
                    if j + 2 < EC:
                        gather_lo(e, p, j + 2)
                    elif not last:
                        gather_lo(e + 1, 1 - p, j + 2 - EC)

            for q in range(WCH):
                weights_lo(0, 0, q)
            gather_lo(0, 0, 0)
            for m in range(IT):
                expert_hidden(0, 0, 0, m)
            gather_lo(0, 0, 1)
            with dve.Fori(0, E // 2 - 1) as i:
                expert(2 * i, 0)
                expert(2 * i + 1, 1)
            expert(E - 2, 0)
            expert(E - 1, 1, last=True)

            def combine(n, t):
                c = GT * n + t
                dve.wait_ge(crows[t], 32 * (n + 1))
                dve.scalar_tensor_tensor(out=acc_tile(c), in0=cg[t][:, 0, :], scalar=wcomb[:, 0, bass.ds(c, 1)],
                                         in1=acc_tile(c), op0=ALU.mult, op1=ALU.add).then_inc(cfirst, 1)
                dve.wait_ge(cfirst, c + 1)
                dve.scalar_tensor_tensor(out=acc_tile(c), in0=cg[t][:, 1, :], scalar=wcomb[:, 1, bass.ds(c, 1)],
                                         in1=acc_tile(c), op0=ALU.mult, op1=ALU.add).then_inc(combined, 1)

            with dve.Fori(0, GROUPS) as n:
                for t in range(GT):
                    combine(n, t)


_INS = ["x", "ctx_2048", "g_xattn", "g_ffn", "L0_xattn_time_decay", "L0_xattn_time_first", "L0_ffn_router",
        "L0_ffn_w_up_gate", "L0_ffn_w_down", "L0_ffn_shared_w_up_gate", "L0_ffn_shared_w_down"]


def kernel(**inputs):
    import numpy as np
    import concourse.bacc as bacc
    from concourse.bass_utils import run_bass_kernel_spmd as run

    nc = bacc.Bacc("TRN2", target_bir_lowering=False, num_devices=1)
    arrays, args = {}, []
    for name in _INS:
        a = np.ascontiguousarray(inputs[name])
        arrays[f"in_{name}"] = a
        args.append(nc.dram_tensor(f"in_{name}", a.shape, mybir.dt.from_np(a.dtype), kind="ExternalInput").ap())
    args.append(nc.dram_tensor("out_0", (BATCH, STEPS, D), F32, kind="ExternalOutput").ap())
    build(nc, *args)
    return run(nc, [arrays], core_ids=[0]).results[0]["out_0"]
```

```python
from contextlib import ExitStack

import concourse.bass as bass
from concourse import mybir

F32, F16, U32 = mybir.dt.float32, mybir.dt.float16, mybir.dt.uint32
ALU, ACT, AX = mybir.AluOpType, mybir.ActivationFunctionType, mybir.AxisListType

P = 128
BATCH, STEPS, D = 16, 256, 512
KT = D // P
TILES = BATCH * STEPS // P
GT = 4
GROUPS = TILES // GT
NTOK = TILES * P
SEG = P + 1
E, TOPK, I, J = 8, 2, 352, 1408
CAP = -(-(NTOK * TOPK * 5) // (E * 4))
ET = CAP // P
CH = 256
EC = CAP // CH
IT = -(-I // P)
IM = [min(P, I - P * m) for m in range(IT)]
JT = J // P
EPS = 1e-5
WS = 2.0 ** 7
HS = 2.0 ** 4
TRASH = E * CAP
SLOTS = JT + GT
WCH = 2 * KT + IT
TABS = 6
SPLIT_FIRST = 6
PMADE = 9
MID, LATE = 14, 18
R_PREF, R_PER = 6, 17


def build(nc, x, ctx_in, g_x, g_f, t_decay, t_first, router, w_ug, w_dn, s_ug, s_dn, out):
    es = ExitStack()
    with es:
        def sb(name, shape, dt):
            return es.enter_context(nc.sbuf_tensor(name, shape, dt))

        def pb(name, shape):
            return es.enter_context(nc.psum_tensor(name, shape, F32))

        def sem(name):
            return es.enter_context(nc.semaphore(name))

        xln_d = nc.dram_tensor("xln_d", (NTOK, D), F32, kind="Internal").ap()
        slot_out_d = nc.dram_tensor("slot_out_d", (E * CAP, D), F32, kind="Internal").ap()
        slot_tok_d = nc.dram_tensor("slot_tok_d", (TRASH + TOPK * NTOK, 1), F32, kind="Internal").ap()

        acc = sb("acc", [P, TILES * D], F32)
        wreg = sb("wreg", [P, JT * 3 * 1024], F16)
        hreg = sb("hreg", [P, JT * 2 * 512], F16)
        xT = sb("xT", [P, 2, 2, KT, 512], F16)
        srng = sb("srng", [P, 2, 512], F32)
        wkv = sb("wkv", [P, 7424], F32)
        sU = wreg[:, 0:JT * 2048].rearrange("p (m g h k c) -> p m g h k c", m=JT, g=2, h=2, k=KT)
        sD = wreg[:, JT * 2048:JT * 3072].rearrange("p (j h c) -> p j h c", j=JT, h=2)
        hh = hreg[:, :].rearrange("p (j h t) -> p j h t", j=JT, h=2)
        sst_u = acc[:, 24 * D:32 * D].rearrange("p (r g k c) -> p r g k c", r=4, g=2, k=KT)
        sst_d = acc[:, 21 * D:24 * D].rearrange("p (r c) -> p r c", r=3)

        at = [0]

        def carve(words):
            a = wkv[:, at[0]:at[0] + words]
            at[0] += words
            return a

        ctxb = [carve(D) for _ in range(2)]
        kbuf = carve(D)
        ek = carve(D)
        xln = [carve(D) for _ in range(2)]
        scan_in = carve(2 * KT * SEG).rearrange("p (n k s) -> p n k s", n=2, k=KT)
        scan_out = carve(2 * KT * SEG).rearrange("p (n k s) -> p n k s", n=2, k=KT)
        nd = carve(2 * D).rearrange("p (n k t) -> p n k t", n=2, k=KT)
        decay = carve(KT * SEG).rearrange("p (k s) -> p k s", k=KT)

        UW = 2 * 2 * KT * I
        EW = UW + IT * 2 * D
        ebuf = [wkv[:, 0:EW // 2].bitcast(F16), hreg[:, 0:EW]]
        eU = [b[:, 0:UW].rearrange("p (g h k c) -> p g h k c", g=2, h=2, k=KT) for b in ebuf]
        eD = [b[:, UW:EW].rearrange("p (j h c) -> p j h c", j=IT, h=2) for b in ebuf]
        at[0] = EW // 2
        wst = [carve(D) for _ in range(2)]
        eh = carve(2 * IT * CH).bitcast(F16).rearrange("p (r j h t) -> p r j h t", r=2, j=IT, h=2)
        xg1 = carve(D)
        assert at[0] == 7424
        ostage = [hreg[:, EW + 1024 * r:EW + 1024 * (r + 1)].bitcast(F32) for r in range(2)]
        esr = [srng[:, 0, CH * r:CH * (r + 1)] for r in range(2)]
        xg = [xg1, srng[:, 1, :]]
        xgT = xT[:, 0, :, :, :].rearrange("p h k (r t) -> p r h k t", r=2)
        cg = [wkv[:, 2 * D * r:2 * D * (r + 1)].rearrange("p (n c) -> p n c", n=2) for r in range(4)]

        tab_rows = srng[0:2 * KT, 1, 0:P]
        ident = sb("ident", [P, P], F32)
        pref = sb("pref", [P, 2, P], F16)
        prefw = srng[:, 0, 0:2 * P].rearrange("p (m r) -> p m r", m=2)
        iotae = sb("iotae", [P, E], F32)
        rowid = sb("rowid", [P, TILES], F32)
        e12 = sb("e12", [P, 2, KT], F32)
        gates = sb("gates", [P, 4], F32)
        mhalf = sb("mhalf", [P, 1], F32)
        rt_w = sb("rt_w", [P, 2, KT, E], F16)
        rt_f = sb("rt_f", [P, KT, E], F32)
        bn = sb("bn", [P, 2, 6], F32)
        mv = sb("mv", [P, 2, 2], F32)
        ve = sb("ve", [P, 2], F32)
        rstd = sb("rstd", [P, 2], F32)
        lt = sb("lt", [P, E], F32)
        top8 = sb("top8", [P, 8], F32)
        top8i = sb("top8i", [P, 8], U32)
        topv = sb("topv", [P, TILES * 2], F32)
        topi = sb("topi", [P, TILES * 2], F32)
        wcomb = sb("wcomb", [P, TOPK, TILES], F32)
        cslot = sb("cslot", [P, TILES * 2], U32)
        sidx = sb("sidx", [P, 2 * GT], U32)
        cidx = sb("cidx", [P, 2 * GT], U32)
        stok = sb("stok", [P, GT], F32)
        gidx = sb("gidx", [P, E * ET], U32)
        eidx = sb("eidx", [P, 2, ET], U32)

        oh = sb("oh", [P, 2, GT, E], F32)[:, :, :, :]
        ohs = sb("ohs", [P, GT, E], F16)
        ohx = sb("ohx", [P, GT + 1, E], F16)
        pos = sb("pos", [P, GT, E], F32)
        sprod = sb("sprod", [P, 2, GT, E], F32)
        posk = sb("posk", [P, 2, GT], F32)
        slot = sb("slot", [P, 2, GT], F32)
        trash = sb("trash", [P, 2, GT], F32)
        valid = sb("valid", [P, 2, TILES], F32)
        wtmp = sb("wtmp", [P, 2, TILES], F32)
        tokt = wkv[0:E * ET, EW // 2 + 2 * D:EW // 2 + 2 * D + P]
        zslot = hreg[0:E * ET, 0:2 * P].bitcast(F32)

        PU = [[pb(f"PU{r}{g}", [P, 512]) for g in range(2)] for r in range(2)]
        PD = [pb(f"PD{r}", [P, 512]) for r in range(2)]
        PT = pb("PT", [P, 512])
        PR = pb("PR", [P, 512])

        dve_waits = sem("dve_waits"); pool_waits = sem("pool_waits")
        tab_in = sem("tab_in"); tab_turned = sem("tab_turned")
        const_in = sem("const_in"); pmade = sem("pmade"); tabs = sem("tabs")
        exps = sem("exps"); consts = sem("consts"); rhi = sem("rhi"); rlo = sem("rlo")
        in_loaded = [sem(f"in_loaded{r}") for r in range(2)]
        bn1 = sem("bn1"); var1 = sem("var1"); rstd1 = sem("rstd1")
        k_norm = sem("k_norm"); k_turned = sem("k_turned"); v_turned = sem("v_turned"); v_used = sem("v_used")
        ek_ready = sem("ek_ready"); k1_ready = sem("k1_ready"); k2_ready = sem("k2_ready")
        kv_steps = sem("kv_steps"); nd_ready = sem("nd_ready")
        carried = sem("carried"); scanned = sem("scanned"); summed = sem("summed")
        rcp_done = sem("rcp_done"); y_done = sem("y_done"); y_turned = sem("y_turned"); x2_done = sem("x2_done")
        bn2 = sem("bn2"); var2 = sem("var2"); rstd2 = sem("rstd2"); xln_ready = sem("xln_ready")
        xln_stored = [sem(f"xln_stored{r}") for r in range(2)]
        x_turned = sem("x_turned"); xhi_ready = sem("xhi_ready"); xlo_ready = sem("xlo_ready")
        logits_ready = sem("logits_ready"); logits_taken = sem("logits_taken"); top_steps = sem("top_steps")
        wu_in = [sem(f"wu_in{r}") for r in range(4)]
        wd_in = [sem(f"wd_in{r}") for r in range(3)]
        wu_hi = sem("wu_hi"); wu_lo = sem("wu_lo"); wd_hi = sem("wd_hi"); wd_sc = sem("wd_sc"); wd_lo = sem("wd_lo")
        up_ready = sem("up_ready"); silu_done = sem("silu_done"); h_ready = sem("h_ready")
        hhi_ready = sem("hhi_ready"); hlo_ready = sem("hlo_ready")
        down_ready = sem("down_ready"); down_added = sem("down_added")
        rsteps = sem("rsteps"); pos_ready = sem("pos_ready"); wsteps = sem("wsteps"); tr_steps = sem("tr_steps")
        slots_zeroed = sem("slots_zeroed"); zeros_made = sem("zeros_made"); slots_sent = sem("slots_sent")
        slots_back = sem("slots_back"); slots_turned = sem("slots_turned"); gidx_ready = sem("gidx_ready")
        eidx_ready = sem("eidx_ready")
        gathered = [sem(f"gathered{r}") for r in range(2)]
        xg_turned = sem("xg_turned"); xg_hi = sem("xg_hi"); xg_lo = sem("xg_lo")
        ew_in = [sem(f"ew_in{r}") for r in range(2)]
        ew_hi = sem("ew_hi"); ew_lo = sem("ew_lo")
        eup_ready = sem("eup_ready"); esilu_done = sem("esilu_done"); eh_ready = sem("eh_ready")
        ehhi_ready = sem("ehhi_ready"); ehlo_ready = sem("ehlo_ready")
        edown_ready = sem("edown_ready"); ostaged = sem("ostaged")
        ostored = [sem(f"ostored{r}") for r in range(2)]
        cidx_copied = sem("cidx_copied")
        crows = [sem(f"crows{r}") for r in range(4)]
        cfirst = sem("cfirst"); combined = sem("combined"); out_stored = sem("out_stored")

        def acc_tile(c):
            return acc[:, bass.ds(c * D, D)]

        block = es.enter_context(nc.Block())

        x_rows, ctx_rows, out_rows = (t.rearrange("b t d -> (b t) d") for t in (x, ctx_in, out))

        def ups_at(gs, step):
            if gs is None:
                return [step // 2] if step >= 0 and step % 2 == 0 and step // 2 < SPLIT_FIRST else []
            return [step + SPLIT_FIRST] if isinstance(gs, int) and gs == 0 and step + SPLIT_FIRST < JT else []

        def tiles_at(stage, step, last=False):
            return ([k for k in range(GT) if 3 * (k - 1) + stage == step] +
                    [GT + k for k in range(2) if SLOTS + 3 * (k - 1) + stage == step and not last])

        def steps_of(first):
            return range(-5 if first else 0, SLOTS)

        @block.sync
        def _(sp):
            def load_tile(c, r):
                sp.dma_start(acc_tile(c), x_rows[bass.ds(c * P, P), :]).then_inc(in_loaded[r], 16)
                sp.dma_start(ctxb[r], ctx_rows[bass.ds(c * P, P), :]).then_inc(in_loaded[r], 16)

            def attn_group(g, last=False):
                for k in range(GT):
                    c = GT * g + k
                    sp.wait_ge(v_turned, c + 1)
                    if not (last and k >= GT - 2):
                        load_tile(c + 2, k % 2)
                    sp.wait_ge(xln_ready, c + 1)
                    sp.dma_start(xln_d[bass.ds(c * P, P), :], xln[k % 2]).then_inc(xln_stored[k % 2], 16)

            for r in range(2):
                sp.sem_inc(ostored[r], 16)
            load_tile(0, 0)
            load_tile(1, 1)
            with sp.Fori(0, GROUPS - 1) as n:
                attn_group(n)
            attn_group(GROUPS - 1, last=True)

            sp.wait_ge(slots_sent, 16 * TOPK * TILES)
            sp.dma_start(tokt, slot_tok_d[0:E * CAP, :].rearrange("(a b) o -> a (b o)", b=P)).then_inc(slots_back, 16)

            def load_chunk(e, p, q):
                w = WCH * e + q
                r = (p + q) % 2
                if isinstance(e, int) and w < 2:
                    sp.wait_ge(xlo_ready, TILES)
                else:
                    sp.wait_ge(ew_lo, w - 1)
                if q < 2 * KT:
                    k, g = q // 2, q % 2
                    src = w_ug[bass.ds(e, 1), k * P:(k + 1) * P, g * I:(g + 1) * I].rearrange("e k c -> (e k) c")
                    sp.dma_start(wst[r][:, 0:I], src).then_inc(ew_in[r], 16)
                else:
                    j = q - 2 * KT
                    src = w_dn[bass.ds(e, 1), j * P:j * P + IM[j], :].rearrange("e k c -> (e k) c")
                    sp.dma_start(wst[r][0:IM[j], :], src).then_inc(ew_in[r], 16)

            for q in range(WCH):
                load_chunk(0, 0, q)
            for q in range(WCH):
                load_chunk(1, 1, q)
            with sp.Fori(1, E // 2) as i:
                for p in range(2):
                    for q in range(WCH):
                        load_chunk(2 * i + p, p, q)

            with sp.Fori(0, GROUPS) as n:
                sp.wait_ge(combined, GT * n + GT)
                sp.dma_start(out_rows[bass.ds(n * GT * P, GT * P), :].rearrange("(j p) d -> p j d", p=P),
                             acc[:, bass.ds(n * GT * D, GT * D)].rearrange("p (j d) -> p j d", j=GT)).then_inc(out_stored, 16)
            sp.wait_ge(out_stored, 16 * GROUPS)
            for r in range(2):
                sp.wait_ge(ostored[r], 16 * (E * EC + 1))
                sp.wait_ge(xln_stored[r], 16 * TILES // 2)
            sp.wait_ge(slots_sent, 16 * TOPK * TILES)

        @block.gpsimd
        def _(pool):
            made_n = [0]

            def chain(ins):
                made_n[0] += 1
                ins.then_inc(pmade, 1)
                pool.wait_ge(pmade, made_n[0])

            chain(pool.memset(ident[:, :], 0.0))
            chain(pool.affine_select(out=ident[:, :], in_=ident[:, :], compare_op=ALU.not_equal, fill=1.0, base=0,
                                     pattern=[[-1, P]], channel_multiplier=1))
            chain(pool.memset(prefw, 1.0))
            chain(pool.affine_select(out=prefw[:, 0], in_=prefw[:, 0], compare_op=ALU.is_ge, fill=0.0, base=-1,
                                     pattern=[[1, P]], channel_multiplier=-1))
            chain(pool.tensor_copy(pref[:, :, :], prefw))
            chain(pool.iota(iotae[:, :], pattern=[[1, E]], base=0, channel_multiplier=0,
                            allow_small_or_imprecise_dtypes=True))
            chain(pool.iota(rowid[:, :], pattern=[[P, TILES]], base=0, channel_multiplier=1,
                            allow_small_or_imprecise_dtypes=True))
            chain(pool.memset(mhalf[:, :], -0.5))
            chain(pool.memset(ohx[:, 0, :], 0.0))
            pool.memset(zslot, 0.0).then_inc(zeros_made, 1)
            pool.wait_ge(zeros_made, 1)
            pool.dma_start(slot_tok_d[0:E * CAP, :].rearrange("(a b) o -> a (b o)", b=P), zslot).then_inc(slots_zeroed, 16)
            pool.wait_ge(slots_zeroed, 16)
            pool.wait_ge(tabs, TABS)

            def wait_alone(s, v):
                pool.wait_ge(s, v)
                pool.sem_inc(pool_waits, 1)

            def inv_std(n, done_v, done_r, c):
                pool.wait_ge(done_v, c + 1)
                pool.tensor_tensor(rstd[:, n:n + 1], ve[:, n:n + 1], mhalf[:, :], ALU.pow).then_inc(done_r, 1)

            def factors(c, k, first):
                ekv = ek.rearrange("p (k t) -> p k t", k=KT)
                pool.wait_ge(ek_ready, c + 1)
                if not (first and k == 0):
                    pool.wait_ge(scanned, c)
                pool.tensor_tensor(scan_in[:, 1, :, 1:SEG], ekv, e12[:, 0, :].unsqueeze(2).to_broadcast([P, KT, P]),
                                   ALU.mult).then_inc(k1_ready, 1)
                if not (first and k == 0):
                    pool.wait_ge(y_done, c)
                pool.tensor_tensor(nd[:, 1], ekv, e12[:, 1, :].unsqueeze(2).to_broadcast([P, KT, P]),
                                   ALU.mult).then_inc(k2_ready, 1)

            def add_states(c):
                pool.wait_ge(nd_ready, c + 1)
                pool.wait_ge(scanned, c + 1)
                pool.tensor_tensor(nd, nd, scan_out[:, :, :, 0:P], ALU.add).then_inc(summed, 1)

            def send_slots(g, t):
                for k in range(TOPK):
                    pool.indirect_dma_start(
                        out=slot_tok_d, out_offset=bass.IndirectOffsetOnAxis(ap=sidx[:, 2 * t + k:2 * t + k + 1], axis=0),
                        in_=stok[:, t:t + 1], in_offset=None).then_inc(slots_sent, 16)

            def split_down_lo(m):
                pool.wait_ge(wd_hi, m + 1)
                pool.tensor_tensor(sD[:, m, 1], sst_d[:, m % 3], sD[:, m, 0], ALU.subtract).then_inc(wd_lo, 1)

            def attn_group(g, first=False, last=False):
                for s in steps_of(first):
                    for k in tiles_at(-2, s, last):
                        inv_std(0, var1, rstd1, GT * g + k)
                    for k in tiles_at(4, s):
                        inv_std(1, var2, rstd2, GT * g + k)
                    for k in tiles_at(0, s, last):
                        factors(GT * g + k, k, first)
                    for k in tiles_at(2, s, last):
                        add_states(GT * g + k)
                    if first and 0 <= s < JT:
                        split_down_lo(s)
                    if not first and s >= SLOTS - 2:
                        if s == SLOTS - 2:
                            wait_alone(rsteps, R_PER * g)
                        for t in range(2):
                            send_slots(g - 1, 2 * (s - SLOTS + 2) + t)

            attn_group(0, first=True)
            attn_group(1)
            with pool.Fori(1, GROUPS // 2 - 1) as n:
                attn_group(2 * n)
                attn_group(2 * n + 1)
            attn_group(GROUPS - 2)
            attn_group(GROUPS - 1, last=True)
            pool.wait_ge(rsteps, R_PER * GROUPS)
            for t in range(GT):
                send_slots(GROUPS - 1, t)

            pool.wait_ge(gidx_ready, 1)
            pool.wait_ge(hlo_ready, JT * (GROUPS - 1))
            for r in range(2):
                pool.wait_ge(xln_stored[r], 16 * TILES // 2)

            def gather_expert(e, p, first):
                pool.tensor_copy(eidx[:, p, :], gidx[:, bass.ds(ET * e, ET)]).then_inc(eidx_ready, 1)
                wait_alone(eidx_ready, e + 1)
                for s in range(ET):
                    if not (first and s < 2):
                        wait_alone(xg_turned, ET * e + s - 1)
                    pool.indirect_dma_start(
                        out=xg[s % 2], out_offset=None, in_=xln_d,
                        in_offset=bass.IndirectOffsetOnAxis(ap=eidx[:, p, s:s + 1], axis=0)).then_inc(gathered[s % 2], 16)

            gather_expert(0, 0, True)
            gather_expert(1, 1, False)
            with pool.Fori(1, E // 2) as i:
                gather_expert(2 * i, 0, False)
                gather_expert(2 * i + 1, 1, False)

            for r in range(2):
                pool.wait_ge(ostored[r], 16 * (E * EC + 1))
            pool.wait_ge(edown_ready, ET * E)

            def gather_rows(c, t):
                pool.tensor_copy(cidx[:, 2 * t:2 * t + 2], cslot[:, bass.ds(2 * c, 2)]).then_inc(cidx_copied, 1)
                wait_alone(cidx_copied, c + 1)
                for k in range(TOPK):
                    pool.indirect_dma_start(
                        out=cg[t][:, k, :], out_offset=None, in_=slot_out_d,
                        in_offset=bass.IndirectOffsetOnAxis(ap=cidx[:, 2 * t + k:2 * t + k + 1], axis=0)).then_inc(crows[t], 16)

            for t in range(GT):
                gather_rows(t, t)
            with pool.Fori(1, GROUPS) as n:
                for t in range(GT):
                    pool.wait_ge(combined, GT * n + t + 1 - GT)
                    gather_rows(GT * n + t, t)

        @block.scalar
        def _(act):
            act.dma_start(gates[:, 0:1], g_x.partition_broadcast(P)).then_inc(const_in, 16)
            act.dma_start(gates[:, 1:2], g_f.partition_broadcast(P)).then_inc(const_in, 16)
            for n, t in enumerate((t_first, t_decay)):
                act.dma_start(tab_rows[n * KT:(n + 1) * KT, :], t.rearrange("(k c) -> k c", c=P)).then_inc(tab_in, 16)
            act.dma_start(rt_f[:, :, :], router.rearrange("(k p) e -> p k e", p=P)).then_inc(const_in, 16)
            ug_v = s_ug.rearrange("(k p) (g m c) -> p g m k c", p=P, g=2, m=JT)
            dn_v = s_dn.rearrange("(j p) c -> p j c", p=P)

            def load_u(m):
                for g in range(2):
                    act.dma_start(sst_u[:, m % 4, g], ug_v[:, g, m]).then_inc(wu_in[m % 4], 16)

            def load_d(j):
                act.dma_start(sst_d[:, j % 3], dn_v[:, j]).then_inc(wd_in[j % 3], 16)

            for m in range(4):
                load_u(m)
            for j in range(3):
                load_d(j)

            act.wait_ge(const_in, 16 * 3)
            act.activation(gates[:, 2:4], gates[:, 0:2], ACT.Tanh).then_inc(exps, 1)
            act.wait_ge(consts, 2)
            act.activation(decay[:, :, 1], PR[:, KT:2 * KT], ACT.Exp).then_inc(exps, 1)
            act.wait_ge(exps, 2)
            act.activation(decay[:, :, 2], decay[:, :, 1], ACT.Exp, scale=-1.0).then_inc(exps, 1)
            act.activation(e12[:, :, :], e12[:, :, :], ACT.Exp).then_inc(exps, 1)
            act.activation(rt_w[:, 0], rt_f[:, :, :], ACT.Copy, scale=WS).then_inc(rhi, 1)

            def split_down_hi(m):
                act.wait_ge(wd_in[m % 3], 16 * (m // 3 + 1))
                act.activation(sst_d[:, m % 3], sst_d[:, m % 3], ACT.Copy, scale=WS).then_inc(wd_sc, 1)
                act.wait_ge(wd_sc, m + 1)
                act.activation(sD[:, m, 0], sst_d[:, m % 3], ACT.Copy).then_inc(wd_hi, 1)
                if m >= 1 and m + 2 < JT:
                    act.wait_ge(wd_lo, m)
                    load_d(m + 2)

            def split_up_hi(m):
                act.wait_ge(wu_in[m % 4], 32 * (m // 4 + 1))
                act.activation(sU[:, m, :, 0], sst_u[:, m % 4], ACT.Copy, scale=WS).then_inc(wu_hi, 1)
                if m >= 1 and m + 3 < JT:
                    act.wait_ge(wu_lo, m)
                    load_u(m + 3)

            def exp_k(c, k, first):
                act.wait_ge(k_turned, c + 1)
                if not (first and k == 0):
                    act.wait_ge(k2_ready, c)
                act.activation(ek, PT[:, :], ACT.Exp).then_inc(ek_ready, 1)

            def x_hi(g, k, first, par):
                c = GT * g + k
                act.wait_ge(x_turned, c + 1)
                act.activation(xT[:, par, 0, :, k * P:(k + 1) * P], PT[:, :].rearrange("p (k t) -> p k t", k=KT),
                               ACT.Copy).then_inc(xhi_ready, 1)

            def shared_hidden(g, gpar, m):
                n = JT * g + m
                r = (gpar + m) % 2
                act.wait_ge(up_ready, n + 1)
                if m >= 2:
                    act.wait_ge(hlo_ready, n - 1)
                act.activation(srng[:, r, :], PU[r][0][:, :], ACT.Silu, scale=1.0 / WS).then_inc(silu_done, 1)
                act.wait_ge(h_ready, n + 1)
                act.activation(hh[:, m, 0, :], srng[:, r, :], ACT.Copy).then_inc(hhi_ready, 1)

            def group(gs, ga, gpar, first=False, last=False):
                for s in steps_of(first):
                    if ga is not None:
                        for k in tiles_at(6, s):
                            x_hi(ga, k, first, 1 - gpar)
                        for k in tiles_at(0, s, last):
                            exp_k(GT * ga + k, k, first)
                    for m in ups_at(gs, s):
                        split_up_hi(m)
                    if gs is None:
                        if 0 <= s < JT:
                            split_down_hi(s)
                    elif s < JT:
                        shared_hidden(gs, gpar, s)

            group(None, 0, 1, first=True)
            group(0, 1, 0)
            with act.Fori(0, GROUPS // 2 - 2) as n:
                group(2 * n + 1, 2 * n + 2, 1)
                group(2 * n + 2, 2 * n + 3, 0)
            group(GROUPS - 3, GROUPS - 2, 1)
            group(GROUPS - 2, GROUPS - 1, 0, last=True)
            act.wait_ge(wsteps, 2)
            act.activation(wtmp[:, 1], wtmp[:, 0], ACT.Exp).then_inc(exps, 1)

            def weights_hi(e, p, q, half):
                w = WCH * e + q
                r = (p + q) % 2
                act.wait_ge(ew_in[r], 16 * (WCH * half + (WCH * p + q) // 2 + 1))
                if q < 2 * KT:
                    act.activation(eU[p][:, q % 2, 0, q // 2], wst[r][:, 0:I], ACT.Copy, scale=WS).then_inc(ew_hi, 1)
                else:
                    j = q - 2 * KT
                    act.activation(eD[p][0:IM[j], j, 0], wst[r][0:IM[j], :], ACT.Copy, scale=WS).then_inc(ew_hi, 1)

            def gather_hi(e, p, j):
                cc = EC * e + j
                for t in range(2):
                    act.wait_ge(xg_turned, 2 * cc + t + 1)
                    if not (isinstance(e, int) and cc < 2):
                        act.wait_ge(eup_ready, IT * (cc - 1))
                    T = (PT, PR)[t]
                    act.activation(xgT[:, (p + j) % 2, 0, :, t * P:(t + 1) * P],
                                   T[:, :].rearrange("p (k t) -> p k t", k=KT), ACT.Copy).then_inc(xg_hi, 1)

            def expert_hidden(e, p, j, m):
                cc = EC * e + j
                n = IT * cc + m
                r = (p + j + m) % 2
                M = IM[m]
                act.wait_ge(eup_ready, n + 1)
                if not (isinstance(e, int) and n < 2):
                    act.wait_ge(ehlo_ready, n - 1)
                act.activation(esr[r][0:M, :], PU[r][0][0:M, 0:CH], ACT.Silu, scale=1.0 / WS).then_inc(esilu_done, 1)
                act.wait_ge(eh_ready, n + 1)
                act.activation(eh[0:M, (p + j) % 2, m, 0, :], esr[r][0:M, :], ACT.Copy).then_inc(ehhi_ready, 1)

            def stage_out(e, p, j):
                cc = EC * e + j
                for t in range(2):
                    act.wait_ge(edown_ready, 2 * cc + t + 1)
                    act.wait_ge(ostored[t], 16 * cc + 16)
                    act.activation(ostage[t], PD[t][:, :], ACT.Copy, scale=1.0 / (WS * HS)).then_inc(ostaged, 1)
                for t in range(2):
                    act.wait_ge(ostaged, 2 * cc + t + 1)
                    act.dma_start(slot_out_d[bass.ds((2 * cc + t) * P, P), :], ostage[t]).then_inc(ostored[t], 16)

            def expert(e, p, half, last=False):
                for j in range(EC):
                    for m in range(IT):
                        q = IT * j + m
                        if not last and q < WCH:
                            weights_hi(e + 1, 1 - p, q, half + p)
                        if j + 1 < EC:
                            expert_hidden(e, p, j + 1, m)
                        elif not last:
                            expert_hidden(e + 1, 1 - p, 0, m)
                    if j + 2 < EC:
                        gather_hi(e, p, j + 2)
                    elif not last:
                        gather_hi(e + 1, 1 - p, j + 2 - EC)
                    stage_out(e, p, j)

            for q in range(WCH):
                weights_hi(0, 0, q, 0)
            act.wait_ge(down_added, TILES - GT)
            gather_hi(0, 0, 0)
            for m in range(IT):
                expert_hidden(0, 0, 0, m)
            gather_hi(0, 0, 1)
            with act.Fori(0, E // 2 - 1) as i:
                expert(2 * i, 0, i)
                expert(2 * i + 1, 1, i)
            expert(E - 2, 0, E // 2 - 1)
            expert(E - 1, 1, E // 2 - 1, last=True)
            group(GROUPS - 1, None, 1)

        @block.tensor
        def _(pe):
            def turn(dst, src):
                for kt in range(KT):
                    mm = pe.transpose(dst[:, kt * P:(kt + 1) * P], src[:, kt * P:(kt + 1) * P], ident[:, :])
                return mm


            def turn_k(c, k, first):
                pe.wait_ge(k_norm, c + 1)
                if k == 1:
                    pe.wait_ge(ek_ready, c)
                elif not (first and k == 0):
                    pe.wait_ge(xlo_ready, c if k == GT else c - 1)
                turn(PT, kbuf).then_inc(k_turned, 1)

            def turn_v(c, k, first):
                if k == 1:
                    pe.wait_ge(v_used, c)
                elif not (first and k == 0):
                    pe.wait_ge(logits_taken, c if k == GT else c - 1)
                turn(PR, ctxb[k % 2]).then_inc(v_turned, 1)

            def turn_y(c, k):
                pe.wait_ge(y_done, c + 1)
                if k < GT - 1:
                    pe.wait_ge(ek_ready, c + 2)
                else:
                    pe.wait_ge(xlo_ready, c)
                turn(PT, nd[:, 0].rearrange("p k t -> p (k t)")).then_inc(y_turned, 1)

            def turn_x(c, k):
                pe.wait_ge(xln_ready, c + 1)
                turn(PT, xln[k % 2]).then_inc(x_turned, 1)

            def logits(g, k, par, route):
                c = GT * g + k
                pe.wait_ge(xlo_ready, c + 1)
                if k < GT - 1:
                    pe.wait_ge(v_used, c + 2)
                elif route:
                    pe.wait_ge(rsteps, R_PER * (g - 1) + R_PREF + 1)
                else:
                    pe.wait_ge(logits_taken, c)
                for hl in range(2):
                    for kt in range(KT):
                        mm = pe.matmul(PR[:, 0:2 * E], xT[:, par, hl, kt, k * P:(k + 1) * P], rt_w[:, :, kt, :],
                                       start=(hl == 0 and kt == 0), stop=(hl == 1 and kt == KT - 1))
                mm.then_inc(logits_ready, 1)

            def positions(g, taken):
                pe.wait_ge(rsteps, R_PER * g + R_PREF)
                pe.wait_ge(logits_taken, taken)
                pe.matmul(PR[:, 0:GT * E], pref[:, 0, :], ohs[:, :, :], start=True, stop=False)
                pe.matmul(PR[:, 0:GT * E], pref[:, 1, :], ohx[:, 0:GT, :], start=False, stop=True).then_inc(pos_ready, 1)

            def up_pair(g, gpar, m, split, turns):
                n = JT * g + m
                r = (gpar + m) % 2
                if split:
                    pe.wait_ge(wu_lo, m + 1)
                if m >= 2:
                    pe.wait_ge(h_ready, n - 1)
                done = 0
                for gu in range(2):
                    for kt in range(KT):
                        for a, b in ((0, 0), (0, 1), (1, 0)):
                            for turned in turns.get(done, ()):
                                turned()
                            mm = pe.matmul(PU[r][gu][:, :], sU[:, m, gu, a, kt, :], xT[:, gpar, b, kt, :],
                                           start=(kt == 0 and a + b == 0), stop=(kt == KT - 1 and a == 1))
                            done += 1
                mm.then_inc(up_ready, 1)

            def down_tile(g, t, turns):
                n = GT * g + t
                if t >= 2:
                    pe.wait_ge(down_added, n - 1)
                done = 0
                for j in range(JT):
                    if t == 0:
                        pe.wait_ge(hlo_ready, JT * g + j + 1)
                    for a, b in ((0, 0), (0, 1), (1, 0)):
                        for turned in turns.get(done, ()):
                            turned()
                        mm = pe.matmul(PD[t % 2][:, :], hh[:, j, a, t * P:(t + 1) * P], sD[:, j, b, :],
                                       start=(j == 0 and a + b == 0), stop=(j == JT - 1 and a == 1))
                        done += 1
                mm.then_inc(down_ready, 1)

            def group(gs, ga, gpar, first=False, split=False, last=False):
                if gs is not None:
                    pe.wait_ge(xlo_ready, GT * gs + GT)
                for s in steps_of(first):
                    turns = {0: [], MID: [], LATE: []}
                    if ga is not None:
                        for k in tiles_at(6, s):
                            turns[0].append(lambda k=k: turn_x(GT * ga + k, k))
                        for k in tiles_at(7, s):
                            turns[0].append(lambda k=k: logits(ga, k, 1 - gpar, not first))
                        for k in tiles_at(2, s, last):
                            turns[0].append(lambda k=k: turn_v(GT * ga + k, k, first))
                        for k in tiles_at(4, s):
                            turns[MID].append(lambda k=k: turn_y(GT * ga + k, k))
                        for k in tiles_at(0, s, last):
                            turns[LATE].append(lambda k=k: turn_k(GT * ga + k, k, first))
                        if s == SLOTS - 3 and not first:
                            turns[0].append(lambda: positions(ga - 1, GT * ga + 3))
                        if s == SLOTS - 1 and last:
                            turns[LATE].append(lambda: positions(ga, TILES))
                    if gs is None:
                        for turned in turns[0] + turns[MID] + turns[LATE]:
                            turned()
                    elif s < JT:
                        up_pair(gs, gpar, s, split, turns)
                    else:
                        if split and s == JT:
                            pe.wait_ge(wd_lo, JT)
                        down_tile(gs, s - JT, turns)

            pe.wait_ge(pmade, PMADE)
            pe.wait_ge(tab_in, 32)
            pe.transpose(PR[:, 0:2 * KT], tab_rows, ident[0:2 * KT, 0:2 * KT]).then_inc(tab_turned, 1)
            pe.wait_ge(rlo, 1)
            pe.wait_ge(tabs, TABS)
            group(None, 0, 1, first=True)
            group(0, 1, 0, split=True)
            with pe.Fori(0, GROUPS // 2 - 2) as n:
                group(2 * n + 1, 2 * n + 2, 1)
                group(2 * n + 2, 2 * n + 3, 0)
            group(GROUPS - 3, GROUPS - 2, 1)
            group(GROUPS - 2, GROUPS - 1, 0, last=True)

            def turn_slots(e, p, j):
                cc = EC * e + j
                for t in range(2):
                    s = 2 * j + t
                    pe.wait_ge(gathered[t], 16 * cc + 16)
                    if not isinstance(e, int) or cc > 0:
                        pe.wait_ge(xg_lo, 2 * cc)
                    T = (PT, PR)[t]
                    for kt in range(KT):
                        mm = pe.transpose(T[:, kt * P:(kt + 1) * P], xg[s % 2][:, kt * P:(kt + 1) * P], ident[:, :])
                    mm.then_inc(xg_turned, 1)

            def up_chunk(e, p, j):
                cc = EC * e + j
                if j == 0:
                    pe.wait_ge(ew_lo, WCH * (e + 1))
                pe.wait_ge(xg_lo, 2 * cc + 2)
                for m in range(IT):
                    n = IT * cc + m
                    r = (p + j + m) % 2
                    M = IM[m]
                    if not (isinstance(e, int) and n < 2):
                        pe.wait_ge(eh_ready, n - 1)
                    for gu in range(2):
                        for kt in range(KT):
                            for a, b in ((0, 0), (0, 1), (1, 0)):
                                mm = pe.matmul(PU[r][gu][0:M, 0:CH], eU[p][:, gu, a, kt, m * P:m * P + M],
                                               xgT[:, (p + j) % 2, b, kt, :],
                                               start=(kt == 0 and a + b == 0), stop=(kt == KT - 1 and a == 1))
                    mm.then_inc(eup_ready, 1)

            def down_chunk(e, p, j):
                cc = EC * e + j
                pe.wait_ge(ehlo_ready, IT * (cc + 1))
                for t in range(2):
                    if j > 0:
                        pe.wait_ge(ostaged, 2 * cc)
                    for m in range(IT):
                        M = IM[m]
                        for a, b in ((0, 0), (0, 1), (1, 0)):
                            mm = pe.matmul(PD[t][:, :], eh[0:M, (p + j) % 2, m, a, t * P:(t + 1) * P],
                                           eD[p][0:M, m, b, :],
                                           start=(m == 0 and a + b == 0), stop=(m == IT - 1 and a == 1))
                    mm.then_inc(edown_ready, 1)

            def expert(e, p, last=False):
                for j in range(EC):
                    if j + 1 < EC:
                        up_chunk(e, p, j + 1)
                    elif not last:
                        up_chunk(e + 1, 1 - p, 0)
                    if j + 2 < EC:
                        turn_slots(e, p, j + 2)
                    elif not last:
                        turn_slots(e + 1, 1 - p, j + 2 - EC)
                    down_chunk(e, p, j)

            pe.wait_ge(slots_back, 16)
            pe.wait_ge(rsteps, R_PER * GROUPS)
            pe.transpose(PR[:, 0:E * ET], tokt, ident[0:E * ET, 0:E * ET]).then_inc(slots_turned, 1)
            pe.wait_ge(gidx_ready, 1)
            pe.wait_ge(down_added, TILES - GT)
            turn_slots(0, 0, 0)
            up_chunk(0, 0, 0)
            turn_slots(0, 0, 1)
            with pe.Fori(0, E // 2 - 1) as i:
                expert(2 * i, 0)
                expert(2 * i + 1, 1)
            expert(E - 2, 0)
            expert(E - 1, 1, last=True)
            pe.wait_ge(ostaged, ET * E)
            pe.wait_ge(ehlo_ready, IT * EC * E)
            group(GROUPS - 1, None, 1)

        @block.vector
        def _(dve):
            ntab = [0]

            def tab_step(ins):
                ntab[0] += 1
                ins.then_inc(tabs, 1)
                dve.wait_ge(tabs, ntab[0])

            dve.wait_ge(tab_turned, 1)
            dve.tensor_scalar(e12[:, 1, :], PR[:, 0:KT], 0.0, None, ALU.min).then_inc(consts, 1)
            dve.tensor_scalar(e12[:, 0, :], PR[:, 0:KT], 0.0, -1.0, ALU.max, ALU.mult).then_inc(consts, 1)
            dve.wait_ge(exps, 3)
            tab_step(dve.tensor_copy(decay[:, :, 3:SEG], decay[:, :, 2].unsqueeze(2).to_broadcast([P, KT, SEG - 3])))
            tab_step(dve.tensor_copy(decay[:, :, 1], decay[:, :, 2]))
            tab_step(dve.memset(decay[:, :, 0], 0.0))
            dve.wait_ge(exps, 4)
            tab_step(dve.tensor_scalar(gates[:, 0:1], gates[:, 3:4], 1.0 / (WS * HS), None, ALU.mult))
            dve.wait_ge(rhi, 1)
            dve.scalar_tensor_tensor(out=rt_w[:, 1], in0=rt_f[:, :, :], scalar=WS, in1=rt_w[:, 0],
                                     op0=ALU.mult, op1=ALU.subtract).then_inc(rlo, 1)
            tab_step(dve.memset(lt[:, :], 0.0))
            tab_step(dve.memset(topv[:, :], 0.0))
            assert ntab[0] == TABS

            def wait_alone(s, v):
                dve.wait_ge(s, v)
                dve.sem_inc(dve_waits, 1)

            def stats(c, n, bn_done, var_done):
                dve.bn_stats(bn[:, n, :], acc_tile(c)).then_inc(bn_done, 1)
                wait_alone(bn_done, 2 * c + 1)
                dve.bn_aggr(mv[:, n, :], bn[:, n, :]).then_inc(bn_done, 1)
                dve.wait_ge(bn_done, 2 * c + 2)
                dve.tensor_scalar(ve[:, n:n + 1], mv[:, n, 1:2], EPS, None, ALU.add).then_inc(var_done, 1)

            def stage_a(g, k):
                wait_alone(in_loaded[k % 2], 32 * (2 * g + k // 2 + 1))
                stats(GT * g + k, 0, bn1, var1)

            def stage_b(c, k, first):
                dve.wait_ge(rstd1, c + 1)
                if not (first and k == 0):
                    dve.wait_ge(k_turned, c)
                dve.tensor_scalar(kbuf, acc_tile(c), mv[:, 0, 0:1], rstd[:, 0:1], ALU.subtract, ALU.mult).then_inc(k_norm, 1)

            def stage_g(c, k, first):
                start = k % 2 == 0
                v = PR[:, :].rearrange("p (k t) -> p k t", k=KT)
                if start:
                    dve.memset(scan_in[:, :, :, 0], 0.0).then_inc(carried, 1)
                else:
                    dve.wait_ge(scanned, c)
                    dve.tensor_copy(scan_in[:, :, :, 0], scan_out[:, :, :, P]).then_inc(carried, 1)
                dve.wait_ge(v_turned, c + 1)
                dve.wait_ge(k1_ready, c + 1)
                dve.tensor_tensor(scan_in[:, 0, :, 1:SEG], v, scan_in[:, 1, :, 1:SEG], ALU.mult).then_inc(kv_steps, 1)
                dve.wait_ge(k2_ready, c + 1)
                if not (first and k == 0):
                    dve.wait_ge(y_turned, c)
                dve.tensor_tensor(nd[:, 0], v, nd[:, 1], ALU.mult).then_inc(kv_steps, 1)
                dve.wait_ge(carried, c + 1)
                dve.wait_ge(kv_steps, 2 * c + 2)
                if not (first and k == 0):
                    dve.wait_ge(summed, c)
                if start:
                    dve.tensor_copy(nd[:, 0, :, 0], v[:, :, 0]).then_inc(v_used, 1)
                    dve.memset(nd[:, 1, :, 0], 1.0).then_inc(nd_ready, 1)
                else:
                    dve.sem_inc(v_used, 1)
                    dve.sem_inc(nd_ready, 1)
                for n in range(2):
                    ins = dve.tensor_tensor_scan(scan_out[:, n].rearrange("p k s -> p (k s)"),
                                                 decay.rearrange("p k s -> p (k s)"),
                                                 scan_in[:, n].rearrange("p k s -> p (k s)"), 0.0, ALU.mult, ALU.add)
                ins.then_inc(scanned, 1)

            def stage_d(c):
                wait_alone(summed, c + 1)
                dve.reciprocal(nd[:, 1], nd[:, 1]).then_inc(rcp_done, 1)
                dve.wait_ge(rcp_done, c + 1)
                dve.tensor_tensor(nd[:, 0], nd[:, 0], nd[:, 1], ALU.mult).then_inc(y_done, 1)

            def stage_x(c):
                dve.wait_ge(y_turned, c + 1)
                dve.scalar_tensor_tensor(out=acc_tile(c), in0=PT[:, :], scalar=gates[:, 2:3], in1=acc_tile(c),
                                         op0=ALU.mult, op1=ALU.add).then_inc(x2_done, 1)
                wait_alone(x2_done, c + 1)
                stats(c, 1, bn2, var2)

            def stage_e(g, k, first):
                c = GT * g + k
                dve.wait_ge(rstd2, c + 1)
                if not (first and k < 2):
                    dve.wait_ge(xln_stored[k % 2], 16 * (2 * g + k // 2))
                    dve.wait_ge(x_turned, c - 1)
                dve.tensor_scalar(xln[k % 2], acc_tile(c), mv[:, 1, 0:1], rstd[:, 1:2],
                                  ALU.subtract, ALU.mult).then_inc(xln_ready, 1)

            def stage_f(c, k, par):
                dve.wait_ge(xhi_ready, c + 1)
                dve.tensor_tensor(xT[:, par, 1, :, k * P:(k + 1) * P], PT[:, :].rearrange("p (k t) -> p k t", k=KT),
                                  xT[:, par, 0, :, k * P:(k + 1) * P], ALU.subtract).then_inc(xlo_ready, 1)

            def stage_r(c):
                dve.wait_ge(logits_ready, c + 1)
                dve.tensor_reduce(lt[:, :], PR[:, 0:2 * E].rearrange("p (n e) -> p e n", n=2), AX.X, ALU.add).then_inc(logits_taken, 1)
                wait_alone(logits_taken, c + 1)
                dve.max(top8[:, :], lt[:, :]).then_inc(top_steps, 1)
                wait_alone(top_steps, 4 * c + 1)
                dve.max_index(top8i[:, :], top8[:, :], lt[:, :]).then_inc(top_steps, 1)
                dve.wait_ge(top_steps, 4 * c + 2)
                dve.tensor_copy(topv[:, bass.ds(2 * c, 2)], top8[:, 0:2]).then_inc(top_steps, 1)
                dve.tensor_copy(topi[:, bass.ds(2 * c, 2)], top8i[:, 0:2]).then_inc(top_steps, 1)

            def split_up_lo(m):
                dve.wait_ge(wu_hi, m + 1)
                dve.scalar_tensor_tensor(out=sU[:, m, :, 1], in0=sst_u[:, m % 4], scalar=WS, in1=sU[:, m, :, 0],
                                         op0=ALU.mult, op1=ALU.subtract).then_inc(wu_lo, 1)

            def shared_hidden(g, gpar, m):
                n = JT * g + m
                r = (gpar + m) % 2
                dve.wait_ge(silu_done, n + 1)
                dve.scalar_tensor_tensor(out=srng[:, r, :], in0=PU[r][1][:, :], scalar=HS / WS, in1=srng[:, r, :],
                                         op0=ALU.mult, op1=ALU.mult).then_inc(h_ready, 1)

            def shared_hidden_lo(g, gpar, m):
                n = JT * g + m
                r = (gpar + m) % 2
                dve.wait_ge(hhi_ready, n + 1)
                dve.tensor_tensor(hh[:, m, 1, :], srng[:, r, :], hh[:, m, 0, :], ALU.subtract).then_inc(hlo_ready, 1)

            def add_down(g, t):
                n = GT * g + t
                dve.wait_ge(down_ready, n + 1)
                dve.scalar_tensor_tensor(out=acc_tile(n), in0=PD[t % 2][:, :], scalar=gates[:, 0:1], in1=acc_tile(n),
                                         op0=ALU.mult, op1=ALU.add).then_inc(down_added, 1)


            def step(g, n, ins):
                ins.then_inc(rsteps, 1)
                wait_alone(rsteps, R_PER * g + n)

            def route_choices(g):
                wait_alone(top_steps, 4 * GT * (g + 1))
                for k in range(TOPK):
                    step(g, 1 + k, dve.tensor_tensor(
                        oh[:, k], topi[:, bass.ds(2 * GT * g, 2 * GT)].rearrange("p (t n) -> p n t", n=2)[:, k].unsqueeze(2)
                        .to_broadcast([P, GT, E]), iotae[:, :].unsqueeze(1).to_broadcast([P, GT, E]), ALU.is_equal))
                step(g, 3, dve.tensor_tensor(ohs[:, :, :], oh[:, 0], oh[:, 1], ALU.add))
                dve.tensor_tensor(ohx[:, 1], ohx[:, 0], ohs[:, 0], ALU.add).then_inc(rsteps, 1)
                dve.wait_ge(rsteps, R_PER * g + 4)
                dve.tensor_tensor(ohx[:, 2], ohx[:, 1], ohs[:, 1], ALU.add).then_inc(rsteps, 1)
                dve.wait_ge(rsteps, R_PER * g + 5)
                dve.tensor_tensor(ohx[:, 3], ohx[:, 2], ohs[:, 2], ALU.add).then_inc(rsteps, 1)
                dve.wait_ge(rsteps, R_PER * g + 6)

            def route_slots(g, first):
                wait_alone(pos_ready, g + 1)
                step(g, 7, dve.tensor_copy(pos[:, :, :], PR[:, 0:GT * E].rearrange("p (t e) -> p t e", e=E)))
                step(g, 8, dve.tensor_tensor(ohx[:, 0], ohx[:, 3], ohs[:, 3], ALU.add))
                for k in range(TOPK):
                    step(g, 9 + k, dve.tensor_tensor(sprod[:, k], oh[:, k], pos[:, :, :], ALU.mult))
                step(g, 11, dve.tensor_reduce(posk[:, :, :], sprod[:, :, :, :], AX.X, ALU.add))
                vg = valid[:, :, bass.ds(GT * g, GT)]
                tg = topi[:, bass.ds(2 * GT * g, 2 * GT)].rearrange("p (t n) -> p n t", n=2)
                step(g, 12, dve.tensor_scalar(vg, posk[:, :, :], float(CAP), None, ALU.is_lt))
                step(g, 13, dve.tensor_scalar(posk[:, :, :], posk[:, :, :], float(CAP - 1), None, ALU.min))
                step(g, 14, dve.scalar_tensor_tensor(out=slot[:, :, :], in0=tg, scalar=float(CAP), in1=posk[:, :, :],
                                                     op0=ALU.mult, op1=ALU.add))
                step(g, 15, dve.tensor_copy(cslot[:, bass.ds(2 * GT * g, 2 * GT)].rearrange("p (t n) -> p n t", n=2),
                                            slot[:, :, :]))
                if not first:
                    wait_alone(slots_sent, 16 * TOPK * GT * g)
                step(g, 16, dve.tensor_copy(stok[:, :], rowid[:, bass.ds(GT * g, GT)]))
                for k in range(TOPK):
                    dve.tensor_scalar(trash[:, k], stok[:, :], float(TRASH + NTOK * k), None, ALU.add).then_inc(tr_steps, 1)
                wait_alone(tr_steps, 5 * g + 2)
                dve.tensor_tensor(slot[:, :, :], slot[:, :, :], trash[:, :, :], ALU.subtract).then_inc(tr_steps, 1)
                wait_alone(tr_steps, 5 * g + 3)
                dve.tensor_tensor(slot[:, :, :], slot[:, :, :], vg, ALU.mult).then_inc(tr_steps, 1)
                wait_alone(tr_steps, 5 * g + 4)
                dve.tensor_tensor(slot[:, :, :], slot[:, :, :], trash[:, :, :], ALU.add).then_inc(tr_steps, 1)
                wait_alone(tr_steps, 5 * g + 5)
                step(g, 17, dve.tensor_copy(sidx[:, :].rearrange("p (t n) -> p n t", n=2), slot[:, :, :]))

            def group(gs, ga, gpar, first=False, last=False):
                par = 1 - gpar
                for s in steps_of(first):
                    for k in tiles_at(7, s):
                        stage_r(GT * ga + k)
                    for k in tiles_at(6, s):
                        stage_f(GT * ga + k, k, par)
                    for k in tiles_at(5, s):
                        stage_e(ga, k, first)
                    if gs is not None and 1 <= s <= JT:
                        shared_hidden_lo(gs, gpar, s - 1)
                    for k in tiles_at(3, s, last):
                        stage_d(GT * ga + k)
                    for k in tiles_at(-2, s, last):
                        stage_a(ga, k)
                    for k in tiles_at(4, s):
                        stage_x(GT * ga + k)
                    for k in tiles_at(-2, s, last):
                        stage_b(GT * ga + k, k, first)
                    for k in tiles_at(2, s, last):
                        stage_g(GT * ga + k, k, first)
                    if s == SLOTS - 4 and not first:
                        route_choices(ga - 1)
                    if s == SLOTS - 3 and not first:
                        route_slots(ga - 1, isinstance(ga, int) and ga == 1)
                    if s == SLOTS - 1 and last:
                        route_choices(ga)
                        route_slots(ga, False)
                    for m in ups_at(gs, s):
                        split_up_lo(m)
                    if gs is not None:
                        if s < JT:
                            shared_hidden(gs, gpar, s)
                        else:
                            add_down(gs, s - JT)

            group(None, 0, 1, first=True)
            group(0, 1, 0)
            with dve.Fori(0, GROUPS // 2 - 2) as n:
                group(2 * n + 1, 2 * n + 2, 1)
                group(2 * n + 2, 2 * n + 3, 0)
            group(GROUPS - 3, GROUPS - 2, 1)
            group(GROUPS - 2, GROUPS - 1, 0, last=True)

            nw = [0]

            def wstep(ins):
                nw[0] += 1
                ins.then_inc(wsteps, 1)
                dve.wait_ge(wsteps, nw[0])

            tv = topv[:, :].rearrange("p (t n) -> p n t", n=2)
            wstep(dve.tensor_tensor(wtmp[:, 0], tv[:, 1], tv[:, 0], ALU.subtract))
            wstep(dve.tensor_scalar(wtmp[:, 0], wtmp[:, 0], 1.0 / WS, None, ALU.mult))
            dve.wait_ge(exps, 5)
            wstep(dve.tensor_scalar(wtmp[:, 0], wtmp[:, 1], 1.0, None, ALU.add))
            wstep(dve.reciprocal(wcomb[:, 0, :], wtmp[:, 0]))
            wstep(dve.tensor_tensor(wcomb[:, 1, :], wcomb[:, 0, :], wtmp[:, 1], ALU.mult))
            wstep(dve.scalar_tensor_tensor(out=wcomb[:, :, :], in0=wcomb[:, :, :], scalar=gates[:, 3:4],
                                           in1=valid[:, :, :], op0=ALU.mult, op1=ALU.mult))

            def weights_lo(e, p, q):
                w = WCH * e + q
                r = (p + q) % 2
                dve.wait_ge(ew_hi, w + 1)
                if q < 2 * KT:
                    dve.scalar_tensor_tensor(out=eU[p][:, q % 2, 1, q // 2], in0=wst[r][:, 0:I], scalar=WS,
                                             in1=eU[p][:, q % 2, 0, q // 2], op0=ALU.mult, op1=ALU.subtract).then_inc(ew_lo, 1)
                else:
                    j = q - 2 * KT
                    dve.scalar_tensor_tensor(out=eD[p][0:IM[j], j, 1], in0=wst[r][0:IM[j], :], scalar=WS,
                                             in1=eD[p][0:IM[j], j, 0], op0=ALU.mult, op1=ALU.subtract).then_inc(ew_lo, 1)

            def gather_lo(e, p, j):
                for t in range(2):
                    dve.wait_ge(xg_hi, 2 * (EC * e + j) + t + 1)
                    T = (PT, PR)[t]
                    dve.tensor_tensor(xgT[:, (p + j) % 2, 1, :, t * P:(t + 1) * P],
                                      T[:, :].rearrange("p (k t) -> p k t", k=KT),
                                      xgT[:, (p + j) % 2, 0, :, t * P:(t + 1) * P], ALU.subtract).then_inc(xg_lo, 1)

            def expert_hidden(e, p, j, m):
                n = IT * (EC * e + j) + m
                r = (p + j + m) % 2
                M = IM[m]
                dve.wait_ge(esilu_done, n + 1)
                dve.scalar_tensor_tensor(out=esr[r][0:M, :], in0=PU[r][1][0:M, 0:CH], scalar=HS / WS,
                                         in1=esr[r][0:M, :], op0=ALU.mult, op1=ALU.mult).then_inc(eh_ready, 1)
                dve.wait_ge(ehhi_ready, n + 1)
                dve.tensor_tensor(eh[0:M, (p + j) % 2, m, 1, :], esr[r][0:M, :], eh[0:M, (p + j) % 2, m, 0, :],
                                  ALU.subtract).then_inc(ehlo_ready, 1)

            def expert(e, p, last=False):
                for j in range(EC):
                    for m in range(IT):
                        q = IT * j + m
                        if not last and q < WCH:
                            weights_lo(e + 1, 1 - p, q)
                        if j + 1 < EC:
                            expert_hidden(e, p, j + 1, m)
                        elif not last:
                            expert_hidden(e + 1, 1 - p, 0, m)
                    if j + 2 < EC:
                        gather_lo(e, p, j + 2)
                    elif not last:
                        gather_lo(e + 1, 1 - p, j + 2 - EC)

            for q in range(WCH):
                weights_lo(0, 0, q)
            dve.wait_ge(slots_turned, 1)
            dve.tensor_copy(gidx[:, :], PR[:, 0:E * ET]).then_inc(gidx_ready, 1)
            gather_lo(0, 0, 0)
            for m in range(IT):
                expert_hidden(0, 0, 0, m)
            gather_lo(0, 0, 1)
            with dve.Fori(0, E // 2 - 1) as i:
                expert(2 * i, 0)
                expert(2 * i + 1, 1)
            expert(E - 2, 0)
            expert(E - 1, 1, last=True)

            def combine(n, t):
                c = GT * n + t
                dve.wait_ge(crows[t], 32 * (n + 1))
                dve.scalar_tensor_tensor(out=acc_tile(c), in0=cg[t][:, 0, :], scalar=wcomb[:, 0, bass.ds(c, 1)],
                                         in1=acc_tile(c), op0=ALU.mult, op1=ALU.add).then_inc(cfirst, 1)
                dve.wait_ge(cfirst, c + 1)
                dve.scalar_tensor_tensor(out=acc_tile(c), in0=cg[t][:, 1, :], scalar=wcomb[:, 1, bass.ds(c, 1)],
                                         in1=acc_tile(c), op0=ALU.mult, op1=ALU.add).then_inc(combined, 1)

            for s in range(SLOTS):
                if 1 <= s <= JT:
                    shared_hidden_lo(GROUPS - 1, 1, s - 1)
                for c in range(2 * s, min(2 * s + 2, TILES - GT)):
                    combine(c // GT, c % GT)
                if s < JT:
                    shared_hidden(GROUPS - 1, 1, s)
                else:
                    add_down(GROUPS - 1, s - JT)
            for t in range(GT):
                combine(GROUPS - 1, t)


_INS = ["x", "ctx_2048", "g_xattn", "g_ffn", "L0_xattn_time_decay", "L0_xattn_time_first", "L0_ffn_router",
        "L0_ffn_w_up_gate", "L0_ffn_w_down", "L0_ffn_shared_w_up_gate", "L0_ffn_shared_w_down"]


def kernel(**inputs):
    import numpy as np
    import concourse.bacc as bacc
    from concourse.bass_utils import run_bass_kernel_spmd as run

    nc = bacc.Bacc("TRN2", target_bir_lowering=False, num_devices=1)
    arrays, args = {}, []
    for name in _INS:
        a = np.ascontiguousarray(inputs[name])
        arrays[f"in_{name}"] = a
        args.append(nc.dram_tensor(f"in_{name}", a.shape, mybir.dt.from_np(a.dtype), kind="ExternalInput").ap())
    args.append(nc.dram_tensor("out_0", (BATCH, STEPS, D), F32, kind="ExternalOutput").ap())
    build(nc, *args)
    return run(nc, [arrays], core_ids=[0]).results[0]["out_0"]
```

```python
from contextlib import ExitStack

import concourse.bass as bass
from concourse import mybir

F32, F16, U32 = mybir.dt.float32, mybir.dt.float16, mybir.dt.uint32
ALU, ACT, AX = mybir.AluOpType, mybir.ActivationFunctionType, mybir.AxisListType

P = 128
BATCH, STEPS, D = 16, 256, 512
KT = D // P
TILES = BATCH * STEPS // P
GT = 4
GROUPS = TILES // GT
NTOK = TILES * P
SEG = P + 1
E, TOPK, I, J = 8, 2, 352, 1408
CAP = -(-(NTOK * TOPK * 5) // (E * 4))
ET = CAP // P
CH = 256
EC = CAP // CH
IT = -(-I // P)
IM = [min(P, I - P * m) for m in range(IT)]
JT = J // P
EPS = 1e-5
WS = 2.0 ** 7
HS = 2.0 ** 4
TRASH = E * CAP
HT = GT // 2
SLOTS = JT + GT
WCH = 2 * KT + IT
TABS = 6
SPLIT_FIRST = 4
SPLIT_AT = -2
PMADE = 10
COPY = 4 * P * GT
AHEAD = 6
TABLE_AT = 6
MID, LATE = 18, 21
R_PREF, R_PER = 6, 14


def build(nc, x, ctx_in, g_x, g_f, t_decay, t_first, router, w_ug, w_dn, s_ug, s_dn, out):
    es = ExitStack()
    with es:
        def sb(name, shape, dt):
            return es.enter_context(nc.sbuf_tensor(name, shape, dt))

        def pb(name, shape):
            return es.enter_context(nc.psum_tensor(name, shape, F32))

        def sem(name):
            return es.enter_context(nc.semaphore(name))

        xln_d = nc.dram_tensor("xln_d", (NTOK, D), F32, kind="Internal").ap()
        moe_d = nc.dram_tensor("moe_d", (NTOK + 2 * P, D), F32, kind="Internal").ap()
        slot_d = nc.dram_tensor("slot_d", (TRASH + TOPK * NTOK, 2), F32, kind="Internal").ap()

        acc = sb("acc", [P, TILES * D], F32)
        wreg = sb("wreg", [P, JT * 3 * 1024], F16)
        hreg = sb("hreg", [P, JT * 2 * 512], F16)
        xT = sb("xT", [P, 2, 2, KT, 512], F16)
        srng = sb("srng", [P, 2, 512], F32)
        wkv = sb("wkv", [P, 7424], F32)
        sU = wreg[:, 0:JT * 2048].rearrange("p (m g h k c) -> p m g h k c", m=JT, g=2, h=2, k=KT)
        sD = wreg[:, JT * 2048:JT * 3072].rearrange("p (j h c) -> p j h c", j=JT, h=2)
        hh = hreg[:, :].rearrange("p (j h t) -> p j h t", j=JT, h=2)
        sst_u = acc[:, 24 * D:32 * D].rearrange("p (r g k c) -> p r g k c", r=4, g=2, k=KT)
        sst_d = acc[:, 21 * D:24 * D].rearrange("p (r c) -> p r c", r=3)

        at = [0]

        def carve(words):
            a = wkv[:, at[0]:at[0] + words]
            at[0] += words
            return a

        ctxb = [carve(D) for _ in range(2)]
        kbuf = carve(D)
        ek = carve(D)
        xln = [carve(D) for _ in range(2)]
        scan_in = carve(2 * KT * SEG).rearrange("p (n k s) -> p n k s", n=2, k=KT)
        scan_out = carve(2 * KT * SEG).rearrange("p (n k s) -> p n k s", n=2, k=KT)
        nd = carve(2 * D).rearrange("p (n k t) -> p n k t", n=2, k=KT)
        decay = carve(KT * SEG).rearrange("p (k s) -> p k s", k=KT)

        UW = 2 * 2 * KT * I
        EW = UW + IT * 2 * D
        ebuf = [wkv[:, 0:EW // 2].bitcast(F16), hreg[:, 0:EW]]
        eU = [b[:, 0:UW].rearrange("p (g h k c) -> p g h k c", g=2, h=2, k=KT) for b in ebuf]
        eD = [b[:, UW:EW].rearrange("p (j h c) -> p j h c", j=IT, h=2) for b in ebuf]
        at[0] = EW // 2
        wst = [carve(D) for _ in range(2)]
        eh = carve(2 * IT * CH).bitcast(F16).rearrange("p (r j h t) -> p r j h t", r=2, j=IT, h=2)
        xg1 = carve(D)
        assert at[0] == 7424
        ostage = [hreg[:, EW + 1024 * r:EW + 1024 * (r + 1)].bitcast(F32) for r in range(2)]
        esr = [srng[:, 0, CH * r:CH * (r + 1)] for r in range(2)]
        xg = [xg1, srng[:, 1, :]]
        xgT = xT[:, 0, :, :, :].rearrange("p h k (r t) -> p r h k t", r=2)
        sums = wkv[:, 0:HT * D].rearrange("p (j c) -> p j c", j=HT)

        tab_rows = srng[0:2 * KT, 1, 0:P]
        ident = sb("ident", [P, P], F32)
        pref = sb("pref", [P, 2, P], F16)
        prefw = srng[:, 0, 0:2 * P].rearrange("p (m r) -> p m r", m=2)
        iotae = sb("iotae", [P, E], F32)
        rowid = sb("rowid", [P, TILES], F32)
        e12 = sb("e12", [P, 2, KT], F32)
        gates = sb("gates", [P, 4], F32)
        mhalf = sb("mhalf", [P, 1], F32)
        rt_w = sb("rt_w", [P, 2, KT, E], F16)
        rt_f = sb("rt_f", [P, KT, E], F32)
        bn = sb("bn", [P, 2, 6], F32)
        mv = sb("mv", [P, 2, 2], F32)
        ve = sb("ve", [P, 2], F32)
        rstd = sb("rstd", [P, 2], F32)
        lt = sb("lt", [P, E], F32)
        top8 = sb("top8", [P, 8], F32)
        top8i = sb("top8i", [P, 8], U32)
        topv = sb("topv", [P, TILES * 2], F32)
        topi = sb("topi", [P, TILES * 2], F32)
        sidx = sb("sidx", [P, 2 * GT], U32)
        stw = sb("stw", [P, TOPK, GT, 2], F32)
        wexp = sb("wexp", [P, 2, GT], F32)
        zeros = sb("zeros", [P, P], F32)
        gidx = sb("gidx", [P, E * ET], U32)
        didx = sb("didx", [P, E * ET], U32)
        wslot = sb("wslot", [P, E * ET], F32)
        eidx = sb("eidx", [P, 2, 2, ET], U32)

        oh = sb("oh", [P, 2, GT, E], F32)[:, :, :, :]
        ohs = sb("ohs", [P, GT, E], F16)
        ohx = sb("ohx", [P, GT + 1, E], F16)
        pos = sb("pos", [P, GT, E], F32)
        sprod = sb("sprod", [P, 2, GT, E], F32)
        posk = sb("posk", [P, 2, GT], F32)
        slot = sb("slot", [P, 2, GT], F32)
        trash = sb("trash", [P, 2, GT], F32)
        valid = sb("valid", [P, 2, GT], F32)
        tokt = wkv[0:E * ET, EW // 2 + 2 * D:EW // 2 + 2 * D + 2 * P].rearrange("p (s n) -> p s n", n=2)
        zslot = hreg[0:E * ET // 2, 0:8 * P].bitcast(F32).rearrange("p (s n) -> p s n", n=2)

        PU = [[pb(f"PU{r}{g}", [P, 512]) for g in range(2)] for r in range(2)]
        PD = [pb(f"PD{r}", [P, 512]) for r in range(2)]
        PT = pb("PT", [P, 512])
        PR = pb("PR", [P, 512])

        dve_waits = sem("dve_waits"); pool_waits = sem("pool_waits")
        tab_in = sem("tab_in"); tab_turned = sem("tab_turned")
        const_in = sem("const_in"); pmade = sem("pmade"); tabs = sem("tabs")
        exps = sem("exps"); consts = sem("consts"); rhi = sem("rhi"); rlo = sem("rlo")
        x_in = [sem(f"x_in{k}") for k in range(GT)]; v_in = [sem(f"v_in{r}") for r in range(2)]
        bn1 = sem("bn1"); var1 = sem("var1"); rstd1 = sem("rstd1")
        k_norm = sem("k_norm"); k_turned = sem("k_turned"); v_turned = sem("v_turned"); v_used = sem("v_used")
        ek_ready = sem("ek_ready"); k2_ready = sem("k2_ready")
        d_used = sem("d_used"); scanned_d = sem("scanned_d"); summed_d = sem("summed_d"); nd_ready = sem("nd_ready")
        carried = sem("carried"); scanned = sem("scanned"); summed = sem("summed")
        rcp_done = sem("rcp_done"); y_done = sem("y_done"); y_turned = sem("y_turned"); x2_done = sem("x2_done")
        bn2 = sem("bn2"); var2 = sem("var2"); rstd2 = sem("rstd2"); xln_ready = sem("xln_ready")
        xln_stored = [sem(f"xln_stored{r}") for r in range(2)]
        x_turned = sem("x_turned"); xhi_ready = sem("xhi_ready"); xlo_ready = sem("xlo_ready")
        logits_ready = sem("logits_ready"); logits_taken = sem("logits_taken"); top_steps = sem("top_steps")
        wu_in = [sem(f"wu_in{r}") for r in range(4)]
        wd_in = [sem(f"wd_in{r}") for r in range(3)]
        wu_hi = sem("wu_hi"); wu_lo = sem("wu_lo"); wd_hi = sem("wd_hi"); wd_sc = sem("wd_sc"); wd_lo = sem("wd_lo")
        up_ready = sem("up_ready"); silu_done = sem("silu_done"); h_ready = sem("h_ready")
        hhi_ready = sem("hhi_ready"); hlo_ready = sem("hlo_ready")
        down_ready = sem("down_ready"); down_added = sem("down_added")
        rsteps = sem("rsteps"); pos_ready = sem("pos_ready"); diff_ready = sem("diff_ready"); wexp_ready = sem("wexp_ready"); tr_steps = sem("tr_steps")
        slots_zeroed = sem("slots_zeroed"); zeros_made = sem("zeros_made"); slots_sent = sem("slots_sent")
        slots_back = sem("slots_back"); slots_turned = sem("slots_turned"); gidx_ready = sem("gidx_ready")
        eidx_ready = sem("eidx_ready")
        gathered = [sem(f"gathered{r}") for r in range(2)]
        xg_turned = sem("xg_turned"); xg_hi = sem("xg_hi"); xg_lo = sem("xg_lo")
        ew_in = [sem(f"ew_in{r}") for r in range(2)]
        ew_hi = sem("ew_hi"); ew_lo = sem("ew_lo")
        eup_ready = sem("eup_ready"); esilu_done = sem("esilu_done"); eh_ready = sem("eh_ready")
        ehhi_ready = sem("ehhi_ready"); ehlo_ready = sem("ehlo_ready")
        edown_ready = sem("edown_ready"); ostaged = sem("ostaged")
        rows_added = [sem(f"rows_added{r}") for r in range(2)]; stage_free = sem("stage_free"); moe_started = sem("moe_started")
        sums_in = sem("sums_in")
        combined = sem("combined"); out_stored = sem("out_stored")

        def acc_tile(c):
            return acc[:, bass.ds(c * D, D)]

        block = es.enter_context(nc.Block())

        x_rows, ctx_rows, out_rows = (t.rearrange("b t d -> (b t) d") for t in (x, ctx_in, out))

        ug_v = s_ug.rearrange("(k p) (g m c) -> p g m k c", p=P, g=2, m=JT)
        dn_v = s_dn.rearrange("(j p) c -> p j c", p=P)

        def load_u(queue, m):
            for g in range(2):
                queue.dma_start(sst_u[:, m % 4, g], ug_v[:, g, m]).then_inc(wu_in[m % 4], 16)

        def load_d(queue, j):
            queue.dma_start(sst_d[:, j % 3], dn_v[:, j]).then_inc(wd_in[j % 3], 16)

        def ups_at(gs, step):
            if gs is None:
                return [m for m in range(SPLIT_FIRST) if step == m + SPLIT_AT]
            return [step + SPLIT_FIRST] if isinstance(gs, int) and gs == 0 and step + SPLIT_FIRST < JT else []

        def tiles_at(stage, step, last=False):
            return ([k for k in range(GT) if 3 * (k - 1) + stage == step] +
                    [GT + k for k in range(2) if SLOTS + 3 * (k - 1) + stage == step and not last])

        def steps_of(first):
            return range(-6 if first else 0, SLOTS)

        @block.sync
        def _(sp):
            def load_x(c, k):
                sp.dma_start(acc_tile(c), x_rows[bass.ds(c * P, P), :]).then_inc(x_in[k], 16)

            def load_ctx(c, r):
                sp.dma_start(ctxb[r], ctx_rows[bass.ds(c * P, P), :]).then_inc(v_in[r], 16)

            def attn_group(g, sums, last=False):
                for k in range(GT):
                    c = GT * g + k
                    sp.wait_ge(v_turned, c + 1)
                    if not (last and k >= GT - 2):
                        load_ctx(c + 2, k % 2)
                    if not last:
                        load_x(c + GT, k)
                    sp.wait_ge(xln_ready, c + 1)
                    sp.dma_start(xln_d[bass.ds(c * P, P), :], xln[k % 2]).then_inc(xln_stored[k % 2], 16)
                    if k == 0 and sums:
                        start_sums(g - 2)

            def start_sums(g):
                sp.wait_ge(down_added, GT * g + GT)
                sp.dma_start(moe_d[bass.ds(g * GT * P, GT * P), :].rearrange("(j p) d -> p j d", p=P),
                             acc[:, bass.ds(g * GT * D, GT * D)].rearrange("p (j d) -> p j d", j=GT)).then_inc(moe_started, 16)

            for k in range(GT):
                load_x(k, k)
                if k < 2:
                    load_ctx(k, k)
            load_u(sp, 0)
            load_d(sp, 0)
            for m in range(1, 4):
                load_u(sp, m)
                if m < 3:
                    load_d(sp, m)
            attn_group(0, False)
            sp.wait_ge(pmade, PMADE)
            sp.dma_start(moe_d[NTOK - HT * P:NTOK + 2 * P, :].rearrange("(p a) (b c) -> p (a b) c", p=P, c=P),
                         zeros[:, :].unsqueeze(1).to_broadcast([P, (HT + 2) * KT, P])).then_inc(moe_started, 16)
            attn_group(1, False)
            with sp.Fori(2, GROUPS - 1) as n:
                attn_group(n, True)
            attn_group(GROUPS - 1, True, last=True)

            def load_chunk(e, p, q):
                w = WCH * e + q
                r = (p + q) % 2
                if isinstance(e, int) and w < 2:
                    sp.wait_ge(xlo_ready, TILES)
                else:
                    sp.wait_ge(ew_lo, w - 1)
                if q < 2 * KT:
                    k, g = q // 2, q % 2
                    src = w_ug[bass.ds(e, 1), k * P:(k + 1) * P, g * I:(g + 1) * I].rearrange("e k c -> (e k) c")
                    sp.dma_start(wst[r][:, 0:I], src).then_inc(ew_in[r], 16)
                else:
                    j = q - 2 * KT
                    src = w_dn[bass.ds(e, 1), j * P:j * P + IM[j], :].rearrange("e k c -> (e k) c")
                    sp.dma_start(wst[r][0:IM[j], :], src).then_inc(ew_in[r], 16)

            for q in range(WCH):
                load_chunk(0, 0, q)
                if q == 1:
                    start_sums(GROUPS - 2)
            for q in range(WCH):
                load_chunk(1, 1, q)
            with sp.Fori(1, E // 2) as i:
                for p in range(2):
                    for q in range(WCH):
                        load_chunk(2 * i + p, p, q)

            for r in range(2):
                sp.wait_ge(rows_added[r], 16 * E * ET // 2)
            half = NTOK - HT * P
            sp.dma_start(sums, moe_d[half:NTOK, :].rearrange("(j p) d -> p j d", p=P)).then_inc(sums_in, 16)
            for lo in range(0, half, COPY):
                n = min(COPY, half - lo)
                sp.dma_start(out_rows[lo:lo + n, :].rearrange("(p a) d -> p (a d)", p=P),
                             moe_d[lo:lo + n, :].rearrange("(p a) d -> p (a d)", p=P)).then_inc(out_stored, 16)
            for t in range(HT):
                c = TILES - HT + t
                sp.wait_ge(down_added, c + 1)
                sp.dma_start(out_rows[c * P:(c + 1) * P, :], acc[:, c * D:(c + 1) * D]).then_inc(out_stored, 16)
            sp.wait_ge(out_stored, 16 * (-(-half // COPY) + HT))
            sp.wait_ge(moe_started, 16 * (GROUPS + 1))
            for r in range(2):
                sp.wait_ge(xln_stored[r], 16 * TILES // 2)
            sp.wait_ge(slots_sent, 16 * TOPK * TILES)

        @block.gpsimd
        def _(pool):
            made_n = [0]

            def chain(ins):
                made_n[0] += 1
                ins.then_inc(pmade, 1)
                pool.wait_ge(pmade, made_n[0])

            chain(pool.memset(ident[:, :], 0.0))
            chain(pool.affine_select(out=ident[:, :], in_=ident[:, :], compare_op=ALU.not_equal, fill=1.0, base=0,
                                     pattern=[[-1, P]], channel_multiplier=1))
            chain(pool.memset(prefw, 1.0))
            chain(pool.affine_select(out=prefw[:, 0], in_=prefw[:, 0], compare_op=ALU.is_ge, fill=0.0, base=-1,
                                     pattern=[[1, P]], channel_multiplier=-1))
            chain(pool.tensor_copy(pref[:, :, :], prefw))
            chain(pool.iota(iotae[:, :], pattern=[[1, E]], base=0, channel_multiplier=0,
                            allow_small_or_imprecise_dtypes=True))
            chain(pool.iota(rowid[:, :], pattern=[[P, TILES]], base=0, channel_multiplier=1,
                            allow_small_or_imprecise_dtypes=True))
            chain(pool.memset(mhalf[:, :], -0.5))
            chain(pool.memset(ohx[:, 0, :], 0.0))
            chain(pool.memset(zeros[:, :], 0.0))
            pool.memset(zslot, 0.0).then_inc(zeros_made, 1)
            pool.wait_ge(zeros_made, 1)
            pool.iota(zslot[:, :, 0], pattern=[[1, 2 * P]], base=NTOK, channel_multiplier=0,
                      allow_small_or_imprecise_dtypes=True).then_inc(zeros_made, 1)
            pool.wait_ge(zeros_made, 2)
            pool.dma_start(slot_d[0:E * CAP, :].rearrange("(a b) o -> a b o", b=2 * P), zslot).then_inc(slots_zeroed, 16)

            def wait_alone(s, v):
                pool.wait_ge(s, v)
                pool.sem_inc(pool_waits, 1)

            def inv_std(n, done_v, done_r, c):
                pool.wait_ge(done_v, c + 1)
                pool.tensor_tensor(rstd[:, n:n + 1], ve[:, n:n + 1], mhalf[:, :], ALU.pow).then_inc(done_r, 1)

            def factors(c, k, first):
                ekv = ek.rearrange("p (k t) -> p k t", k=KT)
                pool.wait_ge(ek_ready, c + 1)
                if not (first and k == 0):
                    pool.wait_ge(scanned, c)
                pool.tensor_tensor(scan_in[:, 1, :, 1:SEG], ekv, e12[:, 0, :].unsqueeze(2).to_broadcast([P, KT, P]),
                                   ALU.mult)
                if not (first and k == 0):
                    pool.wait_ge(y_done, c)
                pool.tensor_tensor(nd[:, 1], ekv, e12[:, 1, :].unsqueeze(2).to_broadcast([P, KT, P]),
                                   ALU.mult).then_inc(k2_ready, 1)

            def add_states(c):
                pool.wait_ge(d_used, c + 1)
                pool.wait_ge(scanned_d, c + 1)
                pool.tensor_tensor(nd[:, 1], nd[:, 1], scan_out[:, 1, :, 0:P], ALU.add).then_inc(summed_d, 1)
                pool.wait_ge(scanned, c + 1)
                pool.tensor_tensor(nd[:, 0], nd[:, 0], scan_out[:, 0, :, 0:P], ALU.add).then_inc(summed, 1)

            def send_slots(g, t):
                for k in range(TOPK):
                    pool.indirect_dma_start(
                        out=slot_d, out_offset=bass.IndirectOffsetOnAxis(ap=sidx[:, 2 * t + k:2 * t + k + 1], axis=0),
                        in_=stw[:, k, t, :], in_offset=None).then_inc(slots_sent, 16)

            def split_down_lo(m):
                pool.wait_ge(wd_hi, m + 1)
                pool.tensor_tensor(sD[:, m, 1], sst_d[:, m % 3], sD[:, m, 0], ALU.subtract).then_inc(wd_lo, 1)

            def attn_group(g, first=False, last=False):
                for s in steps_of(first):
                    for k in tiles_at(-3, s, last):
                        inv_std(0, var1, rstd1, GT * g + k)
                    for k in tiles_at(4, s):
                        inv_std(1, var2, rstd2, GT * g + k)
                    for k in tiles_at(0, s, last):
                        if first and k == 0:
                            pool.wait_ge(exps, 3)
                        factors(GT * g + k, k, first)
                    for k in tiles_at(2, s, last):
                        add_states(GT * g + k)
                    if first and 0 <= s < JT:
                        split_down_lo(s)
                    if not first and s >= SLOTS - 2:
                        if s == SLOTS - 2:
                            wait_alone(rsteps, R_PER * g)
                        for t in range(2):
                            send_slots(g - 1, 2 * (s - SLOTS + 2) + t)

            attn_group(0, first=True)
            pool.wait_ge(slots_zeroed, 16)
            attn_group(1)
            with pool.Fori(1, GROUPS // 2 - 1) as n:
                attn_group(2 * n)
                attn_group(2 * n + 1)
            attn_group(GROUPS - 2)
            attn_group(GROUPS - 1, last=True)
            pool.wait_ge(rsteps, R_PER * GROUPS)
            for t in range(GT):
                send_slots(GROUPS - 1, t)
            pool.wait_ge(slots_sent, 16 * TOPK * TILES)
            pool.dma_start(tokt, slot_d[0:E * CAP, :].rearrange("(a b) o -> a b o", b=P)).then_inc(slots_back, 16)

            pool.wait_ge(gidx_ready, 3)
            pool.wait_ge(hlo_ready, JT * (GROUPS - 1))
            for r in range(2):
                pool.wait_ge(xln_stored[r], 16 * TILES // 2)
            pool.sem_inc(stage_free, 2)

            def take_indices(e, p):
                pool.tensor_copy(eidx[:, p, 0, :], gidx[:, bass.ds(ET * e, ET)]).then_inc(eidx_ready, 1)
                pool.tensor_copy(eidx[:, p, 1, :], didx[:, bass.ds(ET * e, ET)]).then_inc(eidx_ready, 1)
                wait_alone(eidx_ready, 2 * e + 2)

            def gather_rows(e, p, s, first):
                if not first:
                    wait_alone(xg_turned, ET * e + s - 1)
                pool.indirect_dma_start(
                    out=xg[s % 2], out_offset=None, in_=xln_d,
                    in_offset=bass.IndirectOffsetOnAxis(ap=eidx[:, p, 0, s:s + 1], axis=0)).then_inc(gathered[s % 2], 16)

            def expert(e, p, last=False):
                def retire(s):
                    wait_alone(rows_added[s % 2], 16 * (ET // 2 * e + s // 2 + 1))
                    pool.sem_inc(stage_free, 1)

                for s in range(ET):
                    if s == ET - AHEAD and not last:
                        take_indices(e + 1, 1 - p)
                    if s + AHEAD < ET:
                        gather_rows(e, p, s + AHEAD, False)
                    elif not last:
                        gather_rows(e + 1, 1 - p, s + AHEAD - ET, False)
                    wait_alone(ostaged, ET * e + s + 1)
                    pool.indirect_dma_start(
                        out=moe_d, out_offset=bass.IndirectOffsetOnAxis(ap=eidx[:, p, 1, s:s + 1], axis=0),
                        in_=ostage[s % 2], in_offset=None, compute_op=ALU.add).then_inc(rows_added[s % 2], 16)
                    if s >= 1:
                        retire(s - 1)
                retire(ET - 1)

            take_indices(0, 0)
            for s in range(AHEAD):
                gather_rows(0, 0, s, s < 2)
            pool.wait_ge(moe_started, 16 * (GROUPS + 1))
            with pool.Fori(0, E // 2 - 1) as i:
                expert(2 * i, 0)
                expert(2 * i + 1, 1)
            expert(E - 2, 0)
            expert(E - 1, 1, last=True)

        @block.scalar
        def _(act):
            for n, t in enumerate((t_first, t_decay)):
                act.dma_start(tab_rows[n * KT:(n + 1) * KT, :], t.rearrange("(k c) -> k c", c=P)).then_inc(tab_in, 16)
            act.dma_start(gates[:, 0:1], g_x.partition_broadcast(P)).then_inc(const_in, 16)
            act.dma_start(gates[:, 1:2], g_f.partition_broadcast(P)).then_inc(const_in, 16)
            act.dma_start(rt_f[:, :, :], router.rearrange("(k p) e -> p k e", p=P)).then_inc(const_in, 16)

            act.wait_ge(consts, 2)
            act.activation(decay[:, :, 1], PR[:, KT:2 * KT], ACT.Exp).then_inc(exps, 1)
            act.wait_ge(exps, 1)
            act.activation(decay[:, :, 2], decay[:, :, 1], ACT.Exp, scale=-1.0).then_inc(exps, 1)
            act.activation(e12[:, :, :], e12[:, :, :], ACT.Exp).then_inc(exps, 1)

            def split_down_hi(m):
                act.wait_ge(wd_in[m % 3], 16 * (m // 3 + 1))
                act.activation(sst_d[:, m % 3], sst_d[:, m % 3], ACT.Copy, scale=WS).then_inc(wd_sc, 1)
                act.wait_ge(wd_sc, m + 1)
                act.activation(sD[:, m, 0], sst_d[:, m % 3], ACT.Copy).then_inc(wd_hi, 1)
                if m >= 1 and m + 2 < JT:
                    act.wait_ge(wd_lo, m)
                    load_d(act, m + 2)

            def split_up_hi(m):
                act.wait_ge(wu_in[m % 4], 32 * (m // 4 + 1))
                act.activation(sU[:, m, :, 0], sst_u[:, m % 4], ACT.Copy, scale=WS).then_inc(wu_hi, 1)
                if m >= 1 and m + 3 < JT:
                    act.wait_ge(wu_lo, m)
                    load_u(act, m + 3)

            def exp_k(c, k, first):
                act.wait_ge(k_turned, c + 1)
                if not (first and k == 0):
                    act.wait_ge(k2_ready, c)
                act.activation(ek, PT[:, :], ACT.Exp).then_inc(ek_ready, 1)

            def exp_diff(g):
                act.wait_ge(diff_ready, g + 1)
                act.activation(wexp[:, 1], wexp[:, 0], ACT.Exp, scale=1.0 / WS).then_inc(wexp_ready, 1)

            def x_hi(g, k, first, par):
                c = GT * g + k
                act.wait_ge(x_turned, c + 1)
                act.activation(xT[:, par, 0, :, k * P:(k + 1) * P], PT[:, :].rearrange("p (k t) -> p k t", k=KT),
                               ACT.Copy).then_inc(xhi_ready, 1)

            def shared_hidden(g, gpar, m):
                n = JT * g + m
                r = (gpar + m) % 2
                act.wait_ge(up_ready, n + 1)
                if m >= 2:
                    act.wait_ge(hlo_ready, n - 1)
                act.activation(srng[:, r, :], PU[r][0][:, :], ACT.Silu, scale=1.0 / WS).then_inc(silu_done, 1)
                act.wait_ge(h_ready, n + 1)
                act.activation(hh[:, m, 0, :], srng[:, r, :], ACT.Copy).then_inc(hhi_ready, 1)

            def group(gs, ga, gpar, first=False, last=False):
                for s in steps_of(first):
                    if ga is not None:
                        for k in tiles_at(6, s):
                            x_hi(ga, k, first, 1 - gpar)
                        for k in tiles_at(0, s, last):
                            exp_k(GT * ga + k, k, first)
                            if first and k == 0:
                                act.wait_ge(const_in, 16 * 3)
                                act.activation(gates[:, 2:4], gates[:, 0:2], ACT.Tanh).then_inc(exps, 1)
                                act.activation(rt_w[:, 0], rt_f[:, :, :], ACT.Copy, scale=WS).then_inc(rhi, 1)
                    if s == SLOTS - 4 and not first:
                        exp_diff(ga - 1)
                    if s == SLOTS - 1 and last:
                        exp_diff(ga)
                    for m in ups_at(gs, s):
                        split_up_hi(m)
                    if gs is None:
                        if 0 <= s < JT:
                            split_down_hi(s)
                    elif s < JT:
                        shared_hidden(gs, gpar, s)

            group(None, 0, 1, first=True)
            act.wait_ge(slots_zeroed, 16)
            group(0, 1, 0)
            with act.Fori(0, GROUPS // 2 - 2) as n:
                group(2 * n + 1, 2 * n + 2, 1)
                group(2 * n + 2, 2 * n + 3, 0)
            group(GROUPS - 3, GROUPS - 2, 1)
            group(GROUPS - 2, GROUPS - 1, 0, last=True)
            def half_hidden(h, also=None):
                for m in range(JT):
                    n = JT * (GROUPS - 1 + h) + m
                    if h == 1 and m == EW // 1024:
                        act.wait_ge(stage_free, 2 + E * ET)
                    act.wait_ge(up_ready, n + 1)
                    if m >= 2:
                        act.wait_ge(hlo_ready, n - 1)
                    act.activation(esr[n % 2], PU[n % 2][0][:, 0:HT * P], ACT.Silu, scale=1.0 / WS).then_inc(silu_done, 1)
                    act.wait_ge(h_ready, n + 1)
                    act.activation(hh[:, m, 0, 0:HT * P], esr[n % 2], ACT.Copy).then_inc(hhi_ready, 1)
                    if also is not None:
                        also(m)

            def weights_hi(e, p, q, half):
                w = WCH * e + q
                r = (p + q) % 2
                act.wait_ge(ew_in[r], 16 * (WCH * half + (WCH * p + q) // 2 + 1))
                if q < 2 * KT:
                    act.activation(eU[p][:, q % 2, 0, q // 2], wst[r][:, 0:I], ACT.Copy, scale=WS).then_inc(ew_hi, 1)
                else:
                    j = q - 2 * KT
                    act.activation(eD[p][0:IM[j], j, 0], wst[r][0:IM[j], :], ACT.Copy, scale=WS).then_inc(ew_hi, 1)

            def gather_hi(e, p, j):
                cc = EC * e + j
                for t in range(2):
                    act.wait_ge(xg_turned, 2 * cc + t + 1)
                    if not (isinstance(e, int) and cc < 2):
                        act.wait_ge(eup_ready, IT * (cc - 1))
                    T = (PT, PR)[t]
                    act.activation(xgT[:, (p + j) % 2, 0, :, t * P:(t + 1) * P],
                                   T[:, :].rearrange("p (k t) -> p k t", k=KT), ACT.Copy).then_inc(xg_hi, 1)

            def expert_hidden(e, p, j, m):
                cc = EC * e + j
                n = IT * cc + m
                r = (p + j + m) % 2
                M = IM[m]
                act.wait_ge(eup_ready, n + 1)
                if not (isinstance(e, int) and n < 2):
                    act.wait_ge(ehlo_ready, n - 1)
                act.activation(esr[r][0:M, :], PU[r][0][0:M, 0:CH], ACT.Silu, scale=1.0 / WS).then_inc(esilu_done, 1)
                act.wait_ge(eh_ready, n + 1)
                act.activation(eh[0:M, (p + j) % 2, m, 0, :], esr[r][0:M, :], ACT.Copy).then_inc(ehhi_ready, 1)

            def stage_out(e, p, j):
                cc = EC * e + j
                for t in range(2):
                    act.wait_ge(edown_ready, 2 * cc + t + 1)
                    act.wait_ge(stage_free, 2 * cc + t + 1)
                    act.activation(ostage[t], PD[t][:, :], ACT.Copy, scale=wslot[:, bass.ds(2 * cc + t, 1)]).then_inc(ostaged, 1)

            def expert(e, p, half, last=False):
                for j in range(EC):
                    for m in range(IT):
                        q = IT * j + m
                        if not last and q < WCH:
                            weights_hi(e + 1, 1 - p, q, half + p)
                        if j + 1 < EC:
                            expert_hidden(e, p, j + 1, m)
                        elif not last:
                            expert_hidden(e + 1, 1 - p, 0, m)
                    if j + 2 < EC:
                        gather_hi(e, p, j + 2)
                    elif not last:
                        gather_hi(e + 1, 1 - p, j + 2 - EC)
                    stage_out(e, p, j)

            half_hidden(0, lambda q: weights_hi(0, 0, q, 0))
            gather_hi(0, 0, 0)
            act.wait_ge(down_added, TILES - HT)
            act.dma_start(moe_d[NTOK - GT * P:NTOK - HT * P, :].rearrange("(j p) d -> p j d", p=P),
                          acc[:, (TILES - GT) * D:(TILES - HT) * D].rearrange("p (j d) -> p j d", j=HT)).then_inc(moe_started, 16)
            for m in range(IT):
                expert_hidden(0, 0, 0, m)
            gather_hi(0, 0, 1)
            with act.Fori(0, E // 2 - 1) as i:
                expert(2 * i, 0, i)
                expert(2 * i + 1, 1, i)
            expert(E - 2, 0, E // 2 - 1)
            expert(E - 1, 1, E // 2 - 1, last=True)
            half_hidden(1)

        @block.tensor
        def _(pe):
            def turn(dst, src):
                for kt in range(KT):
                    mm = pe.transpose(dst[:, kt * P:(kt + 1) * P], src[:, kt * P:(kt + 1) * P], ident[:, :])
                return mm


            def turn_k(c, k, first):
                pe.wait_ge(k_norm, c + 1)
                if k == 1:
                    pe.wait_ge(ek_ready, c)
                elif not (first and k == 0):
                    pe.wait_ge(xlo_ready, c if k == GT else c - 1)
                turn(PT, kbuf).then_inc(k_turned, 1)

            def turn_v(g, k, first):
                c = GT * g + k
                if k == 1:
                    pe.wait_ge(v_used, c)
                elif first and k == 0:
                    pe.wait_ge(exps, 3)
                else:
                    pe.wait_ge(logits_taken, c if k == GT else c - 1)
                pe.wait_ge(v_in[k % 2], 16 * (2 * g + k // 2 + 1))
                turn(PR, ctxb[k % 2]).then_inc(v_turned, 1)

            def turn_y(c, k):
                pe.wait_ge(y_done, c + 1)
                if k < GT - 1:
                    pe.wait_ge(ek_ready, c + 2)
                else:
                    pe.wait_ge(xlo_ready, c)
                turn(PT, nd[:, 0].rearrange("p k t -> p (k t)")).then_inc(y_turned, 1)

            def turn_x(c, k):
                pe.wait_ge(xln_ready, c + 1)
                turn(PT, xln[k % 2]).then_inc(x_turned, 1)

            def logits(g, k, par, route):
                c = GT * g + k
                pe.wait_ge(xlo_ready, c + 1)
                if isinstance(c, int) and c == 0:
                    pe.wait_ge(rlo, 1)
                if k < GT - 1:
                    pe.wait_ge(v_used, c + 2)
                elif route:
                    pe.wait_ge(rsteps, R_PER * (g - 1) + R_PREF + 1)
                else:
                    pe.wait_ge(logits_taken, c)
                for hl in range(2):
                    for kt in range(KT):
                        mm = pe.matmul(PR[:, 0:2 * E], xT[:, par, hl, kt, k * P:(k + 1) * P], rt_w[:, :, kt, :],
                                       start=(hl == 0 and kt == 0), stop=(hl == 1 and kt == KT - 1))
                mm.then_inc(logits_ready, 1)

            def positions(g, taken):
                pe.wait_ge(rsteps, R_PER * g + R_PREF)
                pe.wait_ge(logits_taken, taken)
                pe.matmul(PR[:, 0:GT * E], pref[:, 0, :], ohs[:, :, :], start=True, stop=False)
                pe.matmul(PR[:, 0:GT * E], pref[:, 1, :], ohx[:, 0:GT, :], start=False, stop=True).then_inc(pos_ready, 1)

            def up_pair(g, gpar, m, split, attend):
                n = JT * g + m
                r = (gpar + m) % 2
                if split:
                    pe.wait_ge(wu_lo, m + 1)
                if m >= 2:
                    pe.wait_ge(h_ready, n - 1)
                done = 0
                for gu in range(2):
                    for kt in range(KT):
                        for a, b in ((0, 0), (0, 1), (1, 0)):
                            attend(done)
                            mm = pe.matmul(PU[r][gu][:, :], sU[:, m, gu, a, kt, :], xT[:, gpar, b, kt, :],
                                           start=(kt == 0 and a + b == 0), stop=(kt == KT - 1 and a == 1))
                            done += 1
                mm.then_inc(up_ready, 1)

            def down_tile(g, t, attend):
                n = GT * g + t
                if t >= 2:
                    pe.wait_ge(down_added, n - 1)
                done = 0
                for j in range(JT):
                    if t == 0:
                        pe.wait_ge(hlo_ready, JT * g + j + 1)
                    for a, b in ((0, 0), (0, 1), (1, 0)):
                        attend(done)
                        mm = pe.matmul(PD[t % 2][:, :], hh[:, j, a, t * P:(t + 1) * P], sD[:, j, b, :],
                                       start=(j == 0 and a + b == 0), stop=(j == JT - 1 and a == 1))
                        done += 1
                mm.then_inc(down_ready, 1)

            def attention(ga, par, s, done, first, last):
                if done == 0:
                    for k in tiles_at(6, s):
                        turn_x(GT * ga + k, k)
                    for k in tiles_at(7, s):
                        logits(ga, k, par, not first)
                    for k in tiles_at(2, s, last):
                        turn_v(ga, k, first)
                    if s == SLOTS - 3 and not first:
                        positions(ga - 1, GT * ga + 3)
                if done == MID:
                    for k in tiles_at(4, s):
                        turn_y(GT * ga + k, k)
                if done == LATE:
                    for k in tiles_at(0, s, last):
                        turn_k(GT * ga + k, k, first)
                    if s == SLOTS - 1 and last:
                        positions(ga, TILES)

            def group(gs, ga, gpar, first=False, split=False, last=False):
                if gs is not None:
                    pe.wait_ge(xlo_ready, GT * gs + GT)
                for s in steps_of(first):
                    def attend(done):
                        attention(ga, 1 - gpar, s, done, first, last)

                    if gs is None:
                        for done in (0, MID, LATE):
                            attend(done)
                    elif s < JT:
                        up_pair(gs, gpar, s, split, attend)
                    else:
                        if split and s == JT:
                            pe.wait_ge(wd_lo, JT)
                        down_tile(gs, s - JT, attend)

            pe.wait_ge(pmade, PMADE)
            pe.wait_ge(tab_in, 32)
            pe.transpose(PR[:, 0:2 * KT], tab_rows, ident[0:2 * KT, 0:2 * KT]).then_inc(tab_turned, 1)
            group(None, 0, 1, first=True)
            group(0, 1, 0, split=True)
            with pe.Fori(0, GROUPS // 2 - 2) as n:
                group(2 * n + 1, 2 * n + 2, 1)
                group(2 * n + 2, 2 * n + 3, 0)
            group(GROUPS - 3, GROUPS - 2, 1)
            group(GROUPS - 2, GROUPS - 1, 0, last=True)

            def turn_slots(e, p, j):
                cc = EC * e + j
                for t in range(2):
                    s = 2 * j + t
                    pe.wait_ge(gathered[t], 16 * cc + 16)
                    if not isinstance(e, int) or cc > 0:
                        pe.wait_ge(xg_lo, 2 * cc)
                    T = (PT, PR)[t]
                    for kt in range(KT):
                        mm = pe.transpose(T[:, kt * P:(kt + 1) * P], xg[s % 2][:, kt * P:(kt + 1) * P], ident[:, :])
                    mm.then_inc(xg_turned, 1)

            def up_chunk(e, p, j):
                cc = EC * e + j
                if j == 0:
                    pe.wait_ge(ew_lo, WCH * (e + 1))
                pe.wait_ge(xg_lo, 2 * cc + 2)
                for m in range(IT):
                    n = IT * cc + m
                    r = (p + j + m) % 2
                    M = IM[m]
                    if not (isinstance(e, int) and n < 2):
                        pe.wait_ge(eh_ready, n - 1)
                    for gu in range(2):
                        for kt in range(KT):
                            for a, b in ((0, 0), (0, 1), (1, 0)):
                                mm = pe.matmul(PU[r][gu][0:M, 0:CH], eU[p][:, gu, a, kt, m * P:m * P + M],
                                               xgT[:, (p + j) % 2, b, kt, :],
                                               start=(kt == 0 and a + b == 0), stop=(kt == KT - 1 and a == 1))
                    mm.then_inc(eup_ready, 1)

            def down_chunk(e, p, j):
                cc = EC * e + j
                pe.wait_ge(ehlo_ready, IT * (cc + 1))
                for t in range(2):
                    if j > 0:
                        pe.wait_ge(ostaged, 2 * cc)
                    for m in range(IT):
                        M = IM[m]
                        for a, b in ((0, 0), (0, 1), (1, 0)):
                            mm = pe.matmul(PD[t][:, :], eh[0:M, (p + j) % 2, m, a, t * P:(t + 1) * P],
                                           eD[p][0:M, m, b, :],
                                           start=(m == 0 and a + b == 0), stop=(m == IT - 1 and a == 1))
                    mm.then_inc(edown_ready, 1)

            def expert(e, p, last=False):
                for j in range(EC):
                    if j + 1 < EC:
                        up_chunk(e, p, j + 1)
                    elif not last:
                        up_chunk(e + 1, 1 - p, 0)
                    if j + 2 < EC:
                        turn_slots(e, p, j + 2)
                    elif not last:
                        turn_slots(e + 1, 1 - p, j + 2 - EC)
                    down_chunk(e, p, j)

            def half_ups(h, also=None):
                for m in range(JT):
                    n = JT * (GROUPS - 1 + h) + m
                    if m >= 2:
                        pe.wait_ge(h_ready, n - 1)
                    for gu in range(2):
                        for kt in range(KT):
                            for a, b in ((0, 0), (0, 1), (1, 0)):
                                mm = pe.matmul(PU[n % 2][gu][:, 0:HT * P], sU[:, m, gu, a, kt, :],
                                               xT[:, 1, b, kt, h * HT * P:(h + 1) * HT * P],
                                               start=(kt == 0 and a + b == 0), stop=(kt == KT - 1 and a == 1))
                    mm.then_inc(up_ready, 1)
                    if also is not None:
                        also(m)

            def half_down(h, t):
                for j in range(JT):
                    if t == 0:
                        pe.wait_ge(hlo_ready, JT * (GROUPS - 1 + h) + j + 1)
                    for a, b in ((0, 0), (0, 1), (1, 0)):
                        mm = pe.matmul(PD[t][:, :], hh[:, j, a, t * P:(t + 1) * P], sD[:, j, b, :],
                                       start=(j == 0 and a + b == 0), stop=(j == JT - 1 and a == 1))
                mm.then_inc(down_ready, 1)

            def turn_table(m):
                if m == TABLE_AT:
                    pe.wait_ge(slots_back, 16)
                    pe.wait_ge(rsteps, R_PER * GROUPS)
                    for n in range(2):
                        pe.transpose(PR[:, n * E * ET:(n + 1) * E * ET], tokt[:, :, n],
                                     ident[0:E * ET, 0:E * ET]).then_inc(slots_turned, 1)

            half_ups(0, turn_table)
            pe.wait_ge(down_added, TILES - GT)
            half_down(0, 0)
            pe.wait_ge(gidx_ready, 3)
            turn_slots(0, 0, 0)
            half_down(0, 1)
            pe.wait_ge(down_added, TILES - HT)
            up_chunk(0, 0, 0)
            turn_slots(0, 0, 1)
            with pe.Fori(0, E // 2 - 1) as i:
                expert(2 * i, 0)
                expert(2 * i + 1, 1)
            expert(E - 2, 0)
            expert(E - 1, 1, last=True)
            pe.wait_ge(ostaged, ET * E)
            pe.wait_ge(ehlo_ready, IT * EC * E)
            half_ups(1)
            for t in range(HT):
                half_down(1, t)

        @block.vector
        def _(dve):
            def wait_alone(s, v):
                dve.wait_ge(s, v)
                dve.sem_inc(dve_waits, 1)

            def decay_table():
                dve.wait_ge(exps, 2)
                dve.tensor_copy(decay[:, :, 3:SEG], decay[:, :, 2].unsqueeze(2).to_broadcast([P, KT, SEG - 3])).then_inc(tabs, 1)
                dve.tensor_copy(decay[:, :, 1], decay[:, :, 2]).then_inc(tabs, 1)
                dve.memset(decay[:, :, 0], 0.0).then_inc(tabs, 1)
                dve.memset(lt[:, :], 0.0).then_inc(tabs, 1)
                dve.memset(topv[:, :], 0.0).then_inc(tabs, 1)
                dve.wait_ge(tabs, TABS - 1)

            def gate_table():
                dve.wait_ge(exps, 4)
                dve.tensor_scalar(gates[:, 0:1], gates[:, 3:4], 1.0 / (WS * HS), None, ALU.mult).then_inc(tabs, 1)
                dve.wait_ge(rhi, 1)
                dve.scalar_tensor_tensor(out=rt_w[:, 1], in0=rt_f[:, :, :], scalar=WS, in1=rt_w[:, 0],
                                         op0=ALU.mult, op1=ALU.subtract).then_inc(rlo, 1)
                dve.wait_ge(tabs, TABS)

            dve.wait_ge(tab_turned, 1)
            dve.tensor_scalar(e12[:, 1, :], PR[:, 0:KT], 0.0, None, ALU.min).then_inc(consts, 1)
            dve.tensor_scalar(e12[:, 0, :], PR[:, 0:KT], 0.0, -1.0, ALU.max, ALU.mult).then_inc(consts, 1)

            def stats(c, n, bn_done, var_done):
                dve.bn_stats(bn[:, n, :], acc_tile(c)).then_inc(bn_done, 1)
                wait_alone(bn_done, 2 * c + 1)
                dve.bn_aggr(mv[:, n, :], bn[:, n, :]).then_inc(bn_done, 1)
                dve.wait_ge(bn_done, 2 * c + 2)
                dve.tensor_scalar(ve[:, n:n + 1], mv[:, n, 1:2], EPS, None, ALU.add).then_inc(var_done, 1)

            def stats_x(g, k):
                wait_alone(x_in[k % GT], 16 * (g + k // GT + 1))
                stats(GT * g + k, 0, bn1, var1)

            def normalise_k(c, k, first):
                dve.wait_ge(rstd1, c + 1)
                if not (first and k == 0):
                    dve.wait_ge(k_turned, c)
                dve.tensor_scalar(kbuf, acc_tile(c), mv[:, 0, 0:1], rstd[:, 0:1], ALU.subtract, ALU.mult).then_inc(k_norm, 1)

            def weigh_and_scan(c, k, first):
                start = k % 2 == 0
                v = PR[:, :].rearrange("p (k t) -> p k t", k=KT)
                dve.wait_ge(k2_ready, c + 1)
                if start:
                    dve.memset(scan_in[:, :, :, 0], 0.0).then_inc(carried, 1)
                    dve.memset(nd[:, 1, :, 0], 1.0).then_inc(nd_ready, 1)
                else:
                    dve.wait_ge(scanned, c)
                    dve.tensor_copy(scan_in[:, :, :, 0], scan_out[:, :, :, P]).then_inc(carried, 1)
                    dve.sem_inc(nd_ready, 1)
                dve.wait_ge(v_turned, c + 1)
                dve.wait_ge(nd_ready, c + 1)
                if not (first and k == 0):
                    dve.wait_ge(y_turned, c)
                dve.tensor_tensor(nd[:, 0], v, nd[:, 1], ALU.mult).then_inc(d_used, 1)
                dve.wait_ge(carried, c + 1)
                for n in (1, 0):
                    if n == 0:
                        dve.tensor_tensor(scan_in[:, 0, :, 1:SEG], v, scan_in[:, 1, :, 1:SEG], ALU.mult).then_inc(v_used, 1)
                        dve.wait_ge(v_used, c + 1)
                    dve.tensor_tensor_scan(scan_out[:, n].rearrange("p k s -> p (k s)"),
                                           decay.rearrange("p k s -> p (k s)"),
                                           scan_in[:, n].rearrange("p k s -> p (k s)"), 0.0,
                                           ALU.mult, ALU.add).then_inc((scanned, scanned_d)[n], 1)

            def divide(c):
                wait_alone(summed_d, c + 1)
                dve.reciprocal(nd[:, 1], nd[:, 1]).then_inc(rcp_done, 1)
                dve.wait_ge(rcp_done, c + 1)
                dve.wait_ge(summed, c + 1)
                dve.tensor_tensor(nd[:, 0], nd[:, 0], nd[:, 1], ALU.mult).then_inc(y_done, 1)

            def add_attention(c):
                dve.wait_ge(y_turned, c + 1)
                dve.scalar_tensor_tensor(out=acc_tile(c), in0=PT[:, :], scalar=gates[:, 2:3], in1=acc_tile(c),
                                         op0=ALU.mult, op1=ALU.add).then_inc(x2_done, 1)
                wait_alone(x2_done, c + 1)
                stats(c, 1, bn2, var2)

            def normalise_x2(g, k, first):
                c = GT * g + k
                dve.wait_ge(rstd2, c + 1)
                if not (first and k < 2):
                    dve.wait_ge(xln_stored[k % 2], 16 * (2 * g + k // 2))
                    dve.wait_ge(x_turned, c - 1)
                dve.tensor_scalar(xln[k % 2], acc_tile(c), mv[:, 1, 0:1], rstd[:, 1:2],
                                  ALU.subtract, ALU.mult).then_inc(xln_ready, 1)

            def x_lo(c, k, par):
                dve.wait_ge(xhi_ready, c + 1)
                dve.tensor_tensor(xT[:, par, 1, :, k * P:(k + 1) * P], PT[:, :].rearrange("p (k t) -> p k t", k=KT),
                                  xT[:, par, 0, :, k * P:(k + 1) * P], ALU.subtract).then_inc(xlo_ready, 1)

            def choose_experts(c):
                dve.wait_ge(logits_ready, c + 1)
                dve.tensor_reduce(lt[:, :], PR[:, 0:2 * E].rearrange("p (n e) -> p e n", n=2), AX.X, ALU.add).then_inc(logits_taken, 1)
                wait_alone(logits_taken, c + 1)
                dve.max(top8[:, :], lt[:, :]).then_inc(top_steps, 1)
                wait_alone(top_steps, 4 * c + 1)
                dve.max_index(top8i[:, :], top8[:, :], lt[:, :]).then_inc(top_steps, 1)
                dve.wait_ge(top_steps, 4 * c + 2)
                dve.tensor_copy(topv[:, bass.ds(2 * c, 2)], top8[:, 0:2]).then_inc(top_steps, 1)
                dve.tensor_copy(topi[:, bass.ds(2 * c, 2)], top8i[:, 0:2]).then_inc(top_steps, 1)

            def split_up_lo(m):
                dve.wait_ge(wu_hi, m + 1)
                dve.scalar_tensor_tensor(out=sU[:, m, :, 1], in0=sst_u[:, m % 4], scalar=WS, in1=sU[:, m, :, 0],
                                         op0=ALU.mult, op1=ALU.subtract).then_inc(wu_lo, 1)

            def shared_hidden(g, gpar, m):
                n = JT * g + m
                r = (gpar + m) % 2
                dve.wait_ge(silu_done, n + 1)
                dve.scalar_tensor_tensor(out=srng[:, r, :], in0=PU[r][1][:, :], scalar=HS / WS, in1=srng[:, r, :],
                                         op0=ALU.mult, op1=ALU.mult).then_inc(h_ready, 1)

            def shared_hidden_lo(g, gpar, m):
                n = JT * g + m
                r = (gpar + m) % 2
                dve.wait_ge(hhi_ready, n + 1)
                dve.tensor_tensor(hh[:, m, 1, :], srng[:, r, :], hh[:, m, 0, :], ALU.subtract).then_inc(hlo_ready, 1)

            def add_down(g, t):
                n = GT * g + t
                dve.wait_ge(down_ready, n + 1)
                dve.scalar_tensor_tensor(out=acc_tile(n), in0=PD[t % 2][:, :], scalar=gates[:, 0:1], in1=acc_tile(n),
                                         op0=ALU.mult, op1=ALU.add).then_inc(down_added, 1)


            def step(g, n, ins):
                ins.then_inc(rsteps, 1)
                wait_alone(rsteps, R_PER * g + n)

            def tstep(g, n, ins):
                ins.then_inc(tr_steps, 1)
                wait_alone(tr_steps, 10 * g + n)

            def route_choices(g):
                wait_alone(top_steps, 4 * GT * (g + 1))
                vg = topv[:, bass.ds(2 * GT * g, 2 * GT)].rearrange("p (t n) -> p n t", n=2)
                dve.tensor_tensor(wexp[:, 0], vg[:, 1], vg[:, 0], ALU.subtract).then_inc(diff_ready, 1)
                for k in range(TOPK):
                    step(g, 1 + k, dve.tensor_tensor(
                        oh[:, k], topi[:, bass.ds(2 * GT * g, 2 * GT)].rearrange("p (t n) -> p n t", n=2)[:, k].unsqueeze(2)
                        .to_broadcast([P, GT, E]), iotae[:, :].unsqueeze(1).to_broadcast([P, GT, E]), ALU.is_equal))
                step(g, 3, dve.tensor_tensor(ohs[:, :, :], oh[:, 0], oh[:, 1], ALU.add))
                dve.tensor_tensor(ohx[:, 1], ohx[:, 0], ohs[:, 0], ALU.add).then_inc(rsteps, 1)
                dve.wait_ge(rsteps, R_PER * g + 4)
                dve.tensor_tensor(ohx[:, 2], ohx[:, 1], ohs[:, 1], ALU.add).then_inc(rsteps, 1)
                dve.wait_ge(rsteps, R_PER * g + 5)
                dve.tensor_tensor(ohx[:, 3], ohx[:, 2], ohs[:, 2], ALU.add).then_inc(rsteps, 1)
                dve.wait_ge(rsteps, R_PER * g + 6)

            def route_slots(g, first):
                wait_alone(pos_ready, g + 1)
                step(g, 7, dve.tensor_copy(pos[:, :, :], PR[:, 0:GT * E].rearrange("p (t e) -> p t e", e=E)))
                step(g, 8, dve.tensor_tensor(ohx[:, 0], ohx[:, 3], ohs[:, 3], ALU.add))
                for k in range(TOPK):
                    step(g, 9 + k, dve.tensor_tensor(sprod[:, k], oh[:, k], pos[:, :, :], ALU.mult))
                step(g, 11, dve.tensor_reduce(posk[:, :, :], sprod[:, :, :, :], AX.X, ALU.add))
                tg = topi[:, bass.ds(2 * GT * g, 2 * GT)].rearrange("p (t n) -> p n t", n=2)
                step(g, 12, dve.tensor_scalar(valid[:, :, :], posk[:, :, :], float(CAP), None, ALU.is_lt))
                step(g, 13, dve.scalar_tensor_tensor(out=slot[:, :, :], in0=tg, scalar=float(CAP), in1=posk[:, :, :],
                                                     op0=ALU.mult, op1=ALU.add))
                if not first:
                    wait_alone(slots_sent, 16 * TOPK * GT * g)
                for k in range(TOPK):
                    dve.tensor_copy(stw[:, k, :, 0], rowid[:, bass.ds(GT * g, GT)]).then_inc(tr_steps, 1)
                    dve.tensor_scalar(trash[:, k], rowid[:, bass.ds(GT * g, GT)], float(TRASH + NTOK * k), None,
                                      ALU.add).then_inc(tr_steps, 1)
                wait_alone(wexp_ready, g + 1)
                tstep(g, 5, dve.tensor_scalar(wexp[:, 0], wexp[:, 1], 1.0, None, ALU.add))
                tstep(g, 6, dve.reciprocal(stw[:, 0, :, 1], wexp[:, 0]))
                dve.tensor_tensor(stw[:, 1, :, 1], stw[:, 0, :, 1], wexp[:, 1], ALU.mult).then_inc(tr_steps, 1)
                tstep(g, 8, dve.tensor_tensor(slot[:, :, :], slot[:, :, :], trash[:, :, :], ALU.subtract))
                tstep(g, 9, dve.tensor_tensor(slot[:, :, :], slot[:, :, :], valid[:, :, :], ALU.mult))
                tstep(g, 10, dve.tensor_tensor(slot[:, :, :], slot[:, :, :], trash[:, :, :], ALU.add))
                step(g, 14, dve.tensor_copy(sidx[:, :].rearrange("p (t n) -> p n t", n=2), slot[:, :, :]))

            def group(gs, ga, gpar, first=False, last=False):
                par = 1 - gpar
                for s in steps_of(first):
                    for k in tiles_at(7, s):
                        choose_experts(GT * ga + k)
                    for k in tiles_at(6, s):
                        x_lo(GT * ga + k, k, par)
                    for k in tiles_at(5, s):
                        normalise_x2(ga, k, first)
                    if gs is not None and 1 <= s <= JT:
                        shared_hidden_lo(gs, gpar, s - 1)
                    for k in tiles_at(-3, s, last):
                        stats_x(ga, k)
                    for k in tiles_at(3, s, last):
                        divide(GT * ga + k)
                    for k in tiles_at(4, s):
                        add_attention(GT * ga + k)
                    for k in tiles_at(-2, s, last):
                        normalise_k(GT * ga + k, k, first)
                    for k in tiles_at(2, s, last):
                        if first and k == 0:
                            decay_table()
                        weigh_and_scan(GT * ga + k, k, first)
                        if first and k == 0:
                            gate_table()
                    if s == SLOTS - 4 and not first:
                        route_choices(ga - 1)
                    if s == SLOTS - 3 and not first:
                        route_slots(ga - 1, isinstance(ga, int) and ga == 1)
                    if s == SLOTS - 1 and last:
                        route_choices(ga)
                        route_slots(ga, False)
                    for m in ups_at(gs, s):
                        split_up_lo(m)
                    if gs is not None:
                        if s < JT:
                            shared_hidden(gs, gpar, s)
                        else:
                            add_down(gs, s - JT)

            group(None, 0, 1, first=True)
            group(0, 1, 0)
            with dve.Fori(0, GROUPS // 2 - 2) as n:
                group(2 * n + 1, 2 * n + 2, 1)
                group(2 * n + 2, 2 * n + 3, 0)
            group(GROUPS - 3, GROUPS - 2, 1)
            group(GROUPS - 2, GROUPS - 1, 0, last=True)

            def weights_lo(e, p, q):
                w = WCH * e + q
                r = (p + q) % 2
                dve.wait_ge(ew_hi, w + 1)
                if q < 2 * KT:
                    dve.scalar_tensor_tensor(out=eU[p][:, q % 2, 1, q // 2], in0=wst[r][:, 0:I], scalar=WS,
                                             in1=eU[p][:, q % 2, 0, q // 2], op0=ALU.mult, op1=ALU.subtract).then_inc(ew_lo, 1)
                else:
                    j = q - 2 * KT
                    dve.scalar_tensor_tensor(out=eD[p][0:IM[j], j, 1], in0=wst[r][0:IM[j], :], scalar=WS,
                                             in1=eD[p][0:IM[j], j, 0], op0=ALU.mult, op1=ALU.subtract).then_inc(ew_lo, 1)

            def gather_lo(e, p, j):
                for t in range(2):
                    dve.wait_ge(xg_hi, 2 * (EC * e + j) + t + 1)
                    T = (PT, PR)[t]
                    dve.tensor_tensor(xgT[:, (p + j) % 2, 1, :, t * P:(t + 1) * P],
                                      T[:, :].rearrange("p (k t) -> p k t", k=KT),
                                      xgT[:, (p + j) % 2, 0, :, t * P:(t + 1) * P], ALU.subtract).then_inc(xg_lo, 1)

            def expert_hidden(e, p, j, m):
                n = IT * (EC * e + j) + m
                r = (p + j + m) % 2
                M = IM[m]
                dve.wait_ge(esilu_done, n + 1)
                dve.scalar_tensor_tensor(out=esr[r][0:M, :], in0=PU[r][1][0:M, 0:CH], scalar=HS / WS,
                                         in1=esr[r][0:M, :], op0=ALU.mult, op1=ALU.mult).then_inc(eh_ready, 1)
                dve.wait_ge(ehhi_ready, n + 1)
                dve.tensor_tensor(eh[0:M, (p + j) % 2, m, 1, :], esr[r][0:M, :], eh[0:M, (p + j) % 2, m, 0, :],
                                  ALU.subtract).then_inc(ehlo_ready, 1)

            def expert(e, p, last=False):
                for j in range(EC):
                    for m in range(IT):
                        q = IT * j + m
                        if not last and q < WCH:
                            weights_lo(e + 1, 1 - p, q)
                        if j + 1 < EC:
                            expert_hidden(e, p, j + 1, m)
                        elif not last:
                            expert_hidden(e + 1, 1 - p, 0, m)
                    if j + 2 < EC:
                        gather_lo(e, p, j + 2)
                    elif not last:
                        gather_lo(e + 1, 1 - p, j + 2 - EC)

            def half_hidden(h, m):
                n = JT * (GROUPS - 1 + h) + m
                dve.wait_ge(silu_done, n + 1)
                dve.scalar_tensor_tensor(out=esr[n % 2], in0=PU[n % 2][1][:, 0:HT * P], scalar=HS / WS, in1=esr[n % 2],
                                         op0=ALU.mult, op1=ALU.mult).then_inc(h_ready, 1)

            def half_hidden_lo(h, m):
                n = JT * (GROUPS - 1 + h) + m
                dve.wait_ge(hhi_ready, n + 1)
                dve.tensor_tensor(hh[:, m, 1, 0:HT * P], esr[n % 2], hh[:, m, 0, 0:HT * P],
                                  ALU.subtract).then_inc(hlo_ready, 1)

            def half_add(h, t):
                n = TILES - GT + HT * h + t
                dve.wait_ge(down_ready, n + 1)
                dve.scalar_tensor_tensor(out=acc_tile(n), in0=PD[t][:, :], scalar=gates[:, 0:1], in1=acc_tile(n),
                                         op0=ALU.mult, op1=ALU.add).then_inc(down_added, 1)

            for m in range(JT):
                half_hidden(0, m)
                half_hidden_lo(0, m)
                weights_lo(0, 0, m)
                if m == TABLE_AT:
                    dve.wait_ge(slots_turned, 2)
                    dve.tensor_scalar(gidx[:, :], PR[:, 0:E * ET], float(NTOK - 1), None, ALU.min).then_inc(gidx_ready, 1)
                    dve.tensor_copy(didx[:, :], PR[:, 0:E * ET]).then_inc(gidx_ready, 1)
                    dve.tensor_scalar(wslot[:, :], PR[:, E * ET:2 * E * ET], gates[:, 0:1], None, ALU.mult).then_inc(gidx_ready, 1)
            half_add(0, 0)
            gather_lo(0, 0, 0)
            half_add(0, 1)
            for m in range(IT):
                expert_hidden(0, 0, 0, m)
            gather_lo(0, 0, 1)
            with dve.Fori(0, E // 2 - 1) as i:
                expert(2 * i, 0)
                expert(2 * i + 1, 1)
            expert(E - 2, 0)
            expert(E - 1, 1, last=True)

            for m in range(JT):
                half_hidden(1, m)
                half_hidden_lo(1, m)
            dve.wait_ge(sums_in, 16)
            for t in range(HT):
                dve.tensor_tensor(acc_tile(TILES - HT + t), sums[:, t], acc_tile(TILES - HT + t), ALU.add).then_inc(combined, 1)
            dve.wait_ge(combined, HT)
            for t in range(HT):
                half_add(1, t)


_INS = ["x", "ctx_2048", "g_xattn", "g_ffn", "L0_xattn_time_decay", "L0_xattn_time_first", "L0_ffn_router",
        "L0_ffn_w_up_gate", "L0_ffn_w_down", "L0_ffn_shared_w_up_gate", "L0_ffn_shared_w_down"]


def kernel(**inputs):
    import numpy as np
    import concourse.bacc as bacc
    from concourse.bass_utils import run_bass_kernel_spmd as run

    nc = bacc.Bacc("TRN2", target_bir_lowering=False, num_devices=1)
    arrays, args = {}, []
    for name in _INS:
        a = np.ascontiguousarray(inputs[name])
        arrays[f"in_{name}"] = a
        args.append(nc.dram_tensor(f"in_{name}", a.shape, mybir.dt.from_np(a.dtype), kind="ExternalInput").ap())
    args.append(nc.dram_tensor("out_0", (BATCH, STEPS, D), F32, kind="ExternalOutput").ap())
    build(nc, *args)
    return run(nc, [arrays], core_ids=[0]).results[0]["out_0"]
```
